# Optimizing a Trainium2 kernel written in Bass

```python
import numpy as np
import jax
import jax.numpy as jnp

def _softmax(x, axis=-1):
    return jax.nn.softmax(x, axis=axis)
def _gelu(x):
    return jax.nn.gelu(x, approximate=True)
def _silu(x):
    return jax.nn.silu(x)
def _sigmoid(x):
    return jax.nn.sigmoid(x)
def _layernorm(x, axis=-1, eps=1e-5):
    m = jnp.mean(x, axis=axis, keepdims=True)
    v = jnp.var(x, axis=axis, keepdims=True)
    return (x - m) / jnp.sqrt(v + eps)
def _scatter_add(tgt, idx, src, axis=0):
    return tgt.at[idx].add(src)
def _segment_sum(src, seg, n):
    return jax.ops.segment_sum(src, seg, n)

kernel_name = 'mk_adj_preln_d2_adj_128_7fbbe4'

def setup_inputs(seed: int = 0):
    np.random.seed(seed)
    _w = jnp.asarray
    def _rec_inputs():
        import jax
        import jax.numpy as jnp
        _gk = jax.random.key(seed)
        x = -0.0005207 + 1.001 * jax.random.normal(jax.random.fold_in(_gk, 1), (16, 1024, 128), jnp.float32)
        _a = jax.random.bernoulli(jax.random.fold_in(_gk, 2), 0.03125, (16, 1024, 1024))
        _a = jnp.logical_or(_a, jnp.swapaxes(_a, -1, -2))
        _a = jnp.logical_or(_a, jnp.eye(1024, dtype=bool))
        _af = _a.astype(jnp.float32)
        _af = _af * jax.random.uniform(jax.random.fold_in(_gk, 3), (16, 1024, 1024), jnp.float32, 0.05, 1)
        adj = _af
        _nm = jnp.ones((16, 1024), dtype=bool)
        nodemask = jnp.where(_nm, 1.0, 0.0).astype(jnp.int32)
        return x, adj, nodemask
    x, adj, nodemask = _rec_inputs()
    def _L0_gnn_setup():
        import jax, jax.numpy as jnp
        import numpy as np
        EPS = 1e-12

        def _adapt_conv(h, edge_weight, W, b, is_last):
            h = h @ W + b
            norm = jnp.linalg.norm(h, axis=-1, keepdims=True)
            nh = h / jnp.maximum(norm, EPS)
            cos = jnp.einsum('bij,bkj->bik', nh, nh)
            ew = edge_weight * cos
            h = jnp.einsum('bpq,bqc->bpc', ew, h)
            if not is_last:
                h = jax.nn.relu(h)
            return h
        key = jax.random.key(seed)
        ks = jax.random.split(key, 8)
        B, N, D, H = (8, 2048, 128, 128)
        s = 1.0 / np.sqrt(D)
        return {'x': jax.random.normal(ks[0], (B, N, D), dtype=jnp.float32), 'edge_weight': jax.random.uniform(ks[1], (B, N, N), dtype=jnp.float32), 'W0': jax.random.normal(ks[2], (D, H), dtype=jnp.float32) * s, 'b0': jnp.zeros((H,), dtype=jnp.float32), 'W1': jax.random.normal(ks[3], (H, H), dtype=jnp.float32) * s, 'b1': jnp.zeros((H,), dtype=jnp.float32), 'W2': jax.random.normal(ks[4], (H, H), dtype=jnp.float32) * s, 'b2': jnp.zeros((H,), dtype=jnp.float32)}
    _L0_gnn_all = _L0_gnn_setup()
    _L0_gnn_in = {k: v for k, v in _L0_gnn_all.items() if k in ('W0', 'b0', 'W1', 'b1', 'W2', 'b2', )}
    del _L0_gnn_all

    def _L1_gnn_setup():
        import jax, jax.numpy as jnp
        import numpy as np
        T_DIL = 10
        K_DIL = 2
        BN_EPS = 1e-05
        NORM_EPS = 1e-12

        def _dilate_pattern(adj_bool, mask_b):
            N = adj_bool.shape[0]

            def step(carry, n):
                row = jnp.take(carry, n, axis=0)
                nbi = row.astype(jnp.int32)
                num = jnp.sum(nbi)
                sf = jnp.where(num > T_DIL, (num + K_DIL - 1) // K_DIL, 1)
                rank = jnp.cumsum(nbi)
                rm = row & (rank % sf == 0)
                valid = (mask_b[n] != 0) & (num > 1)
                rm = jnp.where(valid, rm, False)
                keep = ~rm
                carry = carry.at[n].set(row & keep)
                carry = carry.at[:, n].set(carry[:, n] & keep)
                return (carry, None)
            out, _ = jax.lax.scan(step, adj_bool, jnp.arange(N))
            return out

        def _dilate(adj, mask):
            keep = jax.vmap(_dilate_pattern)(adj > 0, mask)
            return adj * keep.astype(adj.dtype)

        def _sage(x, adj, Wr, Wx, b, mf):
            deg = jnp.clip(jnp.sum(adj, axis=-1, keepdims=True), 1.0, None)
            agg = jnp.einsum('bij,bjd->bid', adj, x) / deg
            out = agg @ Wr + x @ Wx + b
            nrm = jnp.maximum(jnp.linalg.norm(out, axis=-1, keepdims=True), NORM_EPS)
            return out / nrm * mf[..., None]

        def _bn(x, g, b):
            m = jnp.mean(x, axis=(0, 1))
            v = jnp.var(x, axis=(0, 1))
            return (x - m) * jax.lax.rsqrt(v + BN_EPS) * g + b

        def _forward(x, adj, mask, Wr1, Wx1, b1, g1, be1, Wr2, Wx2, b2, g2, be2, Wr3, Wx3, b3, g3, be3, Wl, bl):
            mf = mask.astype(x.dtype)
            adj_d = _dilate(adj, mask)
            h1 = _bn(jax.nn.relu(_sage(x, adj_d, Wr1, Wx1, b1, mf)), g1, be1)
            h2 = _bn(jax.nn.relu(_sage(h1, adj_d, Wr2, Wx2, b2, mf)), g2, be2)
            h3 = _bn(jax.nn.relu(_sage(h2, adj_d, Wr3, Wx3, b3, mf)), g3, be3)
            xc = jnp.concatenate([h1, h2, h3], axis=-1) * mf[..., None]
            return (xc @ Wl + bl) * mf[..., None]
        B, N, D, H, E = (8, 2048, 128, 128, 128)
        key = jax.random.key(seed)
        ks = jax.random.split(key, 24)
        x = jax.random.normal(ks[0], (B, N, D), dtype=jnp.float32)
        a = jax.random.bernoulli(ks[1], 0.01, (B, N, N))
        a = a | jnp.swapaxes(a, 1, 2)
        a = a & ~jnp.eye(N, dtype=bool)[None]
        adj = a.astype(jnp.float32)
        mask = jnp.ones((B, N), dtype=jnp.int32)
        s = 0.05
        p = {}
        dims = [(D, H), (H, H), (H, E)]
        for i, (di, do) in enumerate(dims, 1):
            p[f'Wr{i}'] = s * jax.random.normal(ks[2 * i], (di, do), dtype=jnp.float32)
            p[f'Wx{i}'] = s * jax.random.normal(ks[2 * i + 1], (di, do), dtype=jnp.float32)
            p[f'b{i}'] = jnp.zeros((do,), dtype=jnp.float32)
            p[f'g{i}'] = jnp.ones((do,), dtype=jnp.float32)
            p[f'be{i}'] = jnp.zeros((do,), dtype=jnp.float32)
        p['Wl'] = s * jax.random.normal(ks[10], (2 * H + E, E), dtype=jnp.float32)
        p['bl'] = jnp.zeros((E,), dtype=jnp.float32)
        return {'x': x, 'adj': adj, 'mask': mask, **p}
    _L1_gnn_all = _L1_gnn_setup()
    _L1_gnn_in = {k: v for k, v in _L1_gnn_all.items() if k in ('Wr1', 'Wx1', 'b1', 'g1', 'be1', 'Wr2', 'Wx2', 'b2', 'g2', 'be2', 'Wr3', 'Wx3', 'b3', 'g3', 'be3', 'Wl', 'bl', )}
    del _L1_gnn_all

    return {
        "x": x,
        "adj": adj,
        "nodemask": nodemask,
        "L0_gnn_W0": _L0_gnn_in["W0"],
        "L0_gnn_b0": _L0_gnn_in["b0"],
        "L0_gnn_W1": _L0_gnn_in["W1"],
        "L0_gnn_b1": _L0_gnn_in["b1"],
        "L0_gnn_W2": _L0_gnn_in["W2"],
        "L0_gnn_b2": _L0_gnn_in["b2"],
        "L1_gnn_Wr1": _L1_gnn_in["Wr1"],
        "L1_gnn_Wx1": _L1_gnn_in["Wx1"],
        "L1_gnn_b1": _L1_gnn_in["b1"],
        "L1_gnn_g1": _L1_gnn_in["g1"],
        "L1_gnn_be1": _L1_gnn_in["be1"],
        "L1_gnn_Wr2": _L1_gnn_in["Wr2"],
        "L1_gnn_Wx2": _L1_gnn_in["Wx2"],
        "L1_gnn_b2": _L1_gnn_in["b2"],
        "L1_gnn_g2": _L1_gnn_in["g2"],
        "L1_gnn_be2": _L1_gnn_in["be2"],
        "L1_gnn_Wr3": _L1_gnn_in["Wr3"],
        "L1_gnn_Wx3": _L1_gnn_in["Wx3"],
        "L1_gnn_b3": _L1_gnn_in["b3"],
        "L1_gnn_g3": _L1_gnn_in["g3"],
        "L1_gnn_be3": _L1_gnn_in["be3"],
        "L1_gnn_Wl": _L1_gnn_in["Wl"],
        "L1_gnn_bl": _L1_gnn_in["bl"],
    }

def reference(x, adj, nodemask, L0_gnn_W0, L0_gnn_b0, L0_gnn_W1, L0_gnn_b1, L0_gnn_W2, L0_gnn_b2, L1_gnn_Wr1, L1_gnn_Wx1, L1_gnn_b1, L1_gnn_g1, L1_gnn_be1, L1_gnn_Wr2, L1_gnn_Wx2, L1_gnn_b2, L1_gnn_g2, L1_gnn_be2, L1_gnn_Wr3, L1_gnn_Wx3, L1_gnn_b3, L1_gnn_g3, L1_gnn_be3, L1_gnn_Wl, L1_gnn_bl):
    import jax
    import jax.numpy as jnp
    def _L0_gnn_ref(x, edge_weight, W0, b0, W1, b1, W2, b2):
        import jax, jax.numpy as jnp
        import numpy as np
        EPS = 1e-12

        def _adapt_conv(h, edge_weight, W, b, is_last):
            h = h @ W + b
            norm = jnp.linalg.norm(h, axis=-1, keepdims=True)
            nh = h / jnp.maximum(norm, EPS)
            cos = jnp.einsum('bij,bkj->bik', nh, nh)
            ew = edge_weight * cos
            h = jnp.einsum('bpq,bqc->bpc', ew, h)
            if not is_last:
                h = jax.nn.relu(h)
            return h
        params = [(W0, b0), (W1, b1), (W2, b2)]
        h = x
        n_layers = len(params)
        for i, (W, b) in enumerate(params):
            h = _adapt_conv(h, edge_weight, W, b, is_last=i == n_layers - 1)
        return h

    def _L1_gnn_ref(x, adj, mask, Wr1, Wx1, b1, g1, be1, Wr2, Wx2, b2, g2, be2, Wr3, Wx3, b3, g3, be3, Wl, bl):
        import jax, jax.numpy as jnp
        import numpy as np
        T_DIL = 10
        K_DIL = 2
        BN_EPS = 1e-05
        NORM_EPS = 1e-12

        def _dilate_pattern(adj_bool, mask_b):
            N = adj_bool.shape[0]

            def step(carry, n):
                row = jnp.take(carry, n, axis=0)
                nbi = row.astype(jnp.int32)
                num = jnp.sum(nbi)
                sf = jnp.where(num > T_DIL, (num + K_DIL - 1) // K_DIL, 1)
                rank = jnp.cumsum(nbi)
                rm = row & (rank % sf == 0)
                valid = (mask_b[n] != 0) & (num > 1)
                rm = jnp.where(valid, rm, False)
                keep = ~rm
                carry = carry.at[n].set(row & keep)
                carry = carry.at[:, n].set(carry[:, n] & keep)
                return (carry, None)
            out, _ = jax.lax.scan(step, adj_bool, jnp.arange(N))
            return out

        def _dilate(adj, mask):
            keep = jax.vmap(_dilate_pattern)(adj > 0, mask)
            return adj * keep.astype(adj.dtype)

        def _sage(x, adj, Wr, Wx, b, mf):
            deg = jnp.clip(jnp.sum(adj, axis=-1, keepdims=True), 1.0, None)
            agg = jnp.einsum('bij,bjd->bid', adj, x) / deg
            out = agg @ Wr + x @ Wx + b
            nrm = jnp.maximum(jnp.linalg.norm(out, axis=-1, keepdims=True), NORM_EPS)
            return out / nrm * mf[..., None]

        def _bn(x, g, b):
            m = jnp.mean(x, axis=(0, 1))
            v = jnp.var(x, axis=(0, 1))
            return (x - m) * jax.lax.rsqrt(v + BN_EPS) * g + b

        def _forward(x, adj, mask, Wr1, Wx1, b1, g1, be1, Wr2, Wx2, b2, g2, be2, Wr3, Wx3, b3, g3, be3, Wl, bl):
            mf = mask.astype(x.dtype)
            adj_d = _dilate(adj, mask)
            h1 = _bn(jax.nn.relu(_sage(x, adj_d, Wr1, Wx1, b1, mf)), g1, be1)
            h2 = _bn(jax.nn.relu(_sage(h1, adj_d, Wr2, Wx2, b2, mf)), g2, be2)
            h3 = _bn(jax.nn.relu(_sage(h2, adj_d, Wr3, Wx3, b3, mf)), g3, be3)
            xc = jnp.concatenate([h1, h2, h3], axis=-1) * mf[..., None]
            return (xc @ Wl + bl) * mf[..., None]
        return _forward(x, adj, mask, Wr1, Wx1, b1, g1, be1, Wr2, Wx2, b2, g2, be2, Wr3, Wx3, b3, g3, be3, Wl, bl)

    h = jnp.maximum(_layernorm(x, axis=-1), 0.0)
    x = x + _L0_gnn_ref(h, adj, L0_gnn_W0, L0_gnn_b0, L0_gnn_W1, L0_gnn_b1, L0_gnn_W2, L0_gnn_b2)
    h = jnp.maximum(_layernorm(x, axis=-1), 0.0)
    x = x + _L1_gnn_ref(h, adj, nodemask, L1_gnn_Wr1, L1_gnn_Wx1, L1_gnn_b1, L1_gnn_g1, L1_gnn_be1, L1_gnn_Wr2, L1_gnn_Wx2, L1_gnn_b2, L1_gnn_g2, L1_gnn_be2, L1_gnn_Wr3, L1_gnn_Wx3, L1_gnn_b3, L1_gnn_g3, L1_gnn_be3, L1_gnn_Wl, L1_gnn_bl)
    return x


_drawn_inputs = setup_inputs


def setup_inputs(seed=0):
    import zlib

    import numpy as np

    out = dict(_drawn_inputs(seed))
    spreads = {'L0_gnn_b0': (0.0, 0.1),
     'L0_gnn_b1': (0.0, 0.1),
     'L0_gnn_b2': (0.0, 2.0),
     'L1_gnn_b1': (0.0, 2.0),
     'L1_gnn_g1': (1.0, 0.6),
     'L1_gnn_be1': (0.0, 2.0),
     'L1_gnn_b2': (0.0, 2.0),
     'L1_gnn_g2': (1.0, 0.6),
     'L1_gnn_be2': (0.0, 2.0),
     'L1_gnn_b3': (0.0, 2.0),
     'L1_gnn_g3': (1.0, 0.6),
     'L1_gnn_be3': (0.0, 2.0),
     'L1_gnn_bl': (0.0, 2.0)}
    factors = {'L1_gnn_Wr1': 64.0,
     'L1_gnn_Wx1': 64.0,
     'L1_gnn_Wr2': 64.0,
     'L1_gnn_Wx2': 64.0,
     'L1_gnn_Wr3': 64.0,
     'L1_gnn_Wx3': 64.0,
     'L1_gnn_Wl': 64.0}
    for name, (base, spread) in spreads.items():
        noise = np.random.default_rng([zlib.crc32(name.encode()), seed]).standard_normal(out[name].shape)
        drawn = base * np.exp(spread * noise) if base else spread * noise
        out[name] = jnp.asarray(drawn.astype(out[name].dtype))
    for name, factor in factors.items():
        out[name] = (out[name] * factor).astype(out[name].dtype)
    return out
```

```python
from contextlib import ExitStack

import numpy as np
import concourse.bass as bass
from concourse import mybir

F32 = mybir.dt.float32
F16 = mybir.dt.float16
BF16 = mybir.dt.bfloat16
FP8 = mybir.dt.float8e4
U8 = mybir.dt.uint8
I32 = mybir.dt.int32
ALU = mybir.AluOpType
ACT = mybir.ActivationFunctionType
AXX = mybir.AxisListType.X

G = 16
N = 1024
D = 128
NK = 8
MAGIC = 8388608.0
ONE8 = 56.0
ROUNDS = [3, 3, 5, 7, 7, 5, 3, 8]
ENGINES = ("pe", "act", "dve", "pool", "sp")


class Lane:

    def __init__(self, sem):
        self.sem, self.count, self.todo, self.seen = sem, 0, [], {}


class Phase:

    def __init__(self, nc, ctx, name, sems=None):
        self.nc, self.ctx, self.name = nc, ctx, name
        self.sems = {} if sems is None else sems
        self.lanes = {e: Lane(self.sem(e)) for e in ENGINES}
        self.chans = []

    def sem(self, name):
        if name not in self.sems:
            self.sems[name] = self.ctx.enter_context(self.nc.semaphore(f"{self.name}_{name}"))
        return self.sems[name]

    def sb(self, name, shape, dt=F32):
        return self.ctx.enter_context(self.nc.sbuf_tensor(f"{self.name}_{name}", shape, dt))

    def ps(self, name, shape, dt=F32):
        return self.ctx.enter_context(self.nc.psum_tensor(f"{self.name}_{name}", shape, dt))

    def chan(self, name):
        c = [self.sem(name), 0]
        self.chans.append(c)
        return c

    def _put(self, e, fn, waits, sem, by):
        lane = self.lanes[e]
        need = {}
        for s, v in flat(waits):
            if lane.seen.get(s, 0) < v:
                need[s] = max(need.get(s, 0), v)
        lane.seen.update(need)
        lane.todo.append((list(need.items()), fn, sem, by))

    def op(self, e, fn, *waits, sig=True):
        lane = self.lanes[e]
        if sig:
            lane.count += 1
        self._put(e, fn, waits, lane.sem if sig else None, 1)
        return (lane.sem, lane.count) if sig else None

    def pe(self, fn, *waits, sig=True):
        return self.op("pe", fn, *waits, sig=sig)

    def act(self, fn, *waits):
        return self.op("act", fn, *waits)

    def dve(self, fn, *waits):
        return self.op("dve", fn, *waits)

    def pool(self, fn, *waits):
        return self.op("pool", fn, *waits)

    def dma(self, e, chan, out, in_, *waits):
        chan[1] += 16
        self._put(e, lambda q: q.dma_start(out, in_), waits, chan[0], 16)
        return (chan[0], chan[1])

    def run(self):
        for c in self.chans:
            if c[1]:
                self._put("sp", None, [(c[0], c[1])], None, 0)

        def play(e, eng):
            for need, fn, sem, by in self.lanes[e].todo:
                for s, v in need:
                    eng.wait_ge(s, v)
                if fn is not None:
                    ins = fn(eng)
                    if sem is not None:
                        ins.then_inc(sem, by)

        with self.nc.Block() as block:
            block.tensor(lambda eng: play("pe", eng))
            block.scalar(lambda eng: play("act", eng))
            block.vector(lambda eng: play("dve", eng))
            block.gpsimd(lambda eng: play("pool", eng))
            block.sync(lambda eng: play("sp", eng))


def flat(ws):
    for w in ws:
        if w is None:
            continue
        if isinstance(w, tuple) and len(w) == 2 and isinstance(w[1], int):
            yield w
        else:
            yield from flat(w)


class Buf:

    def __init__(self, t):
        self.t, self.free, self.ready = t, [], None


def bc(ap, n):
    return ap.unsqueeze(2).to_broadcast([ap.shape[0], ap.shape[1], n])


def blk(k):
    return slice(k * 128, k * 128 + 128)


def build(nc, A):
    with ExitStack() as top:
        def sb(name, shape, dt=F32):
            return top.enter_context(nc.sbuf_tensor(name, shape, dt))

        C = {}
        C["ident"] = sb("ident", [128, 128])
        C["ident8"] = sb("ident8", [128, 128], FP8)
        C["tri"] = sb("tri", [128, 128], FP8)
        C["U2"] = sb("U2", [128, 132], BF16)
        C["UL"] = sb("UL", [128, N], BF16)
        C["two1"] = sb("two1", [128, 2], BF16)
        C["zero1"] = sb("zero1", [128, 2], BF16)
        C["onesf"] = sb("onesf", [128, 128])
        C["eps"] = sb("eps", [128, 1])
        C["mi"] = sb("mi", [128, 128], I32)
        C["mf"] = sb("mf", [128, 128])
        C["mv"] = sb("mv", [128, 128])
        C["W"] = sb("W", [128, 12, 128])
        C["rows"] = sb("rows", [128, 13, 128])
        C["cols"] = sb("cols", [128, 6])
        C["flags"] = sb("flags", [128, 128])
        C["flag"] = sb("flag", [128, 1], I32)
        C["rdeg"] = sb("rdeg", [128, G, NK])
        C["rho"] = sb("rho", [128, G, NK])

        S = {}
        for n in ("x1", "z1", "z2", "z3", "ag1", "ag2", "ya", "yb"):
            S[n] = nc.dram_tensor(f"scr_{n}", [G, 128, N], F32, kind="Internal").ap()
        S["keep"] = nc.dram_tensor("scr_keep", [G, NK, 128, N], U8, kind="Internal").ap()

        setup(nc, A, C)
        layer0(nc, A, C, S)
        unsettled = changed(nc, C)
        with nc.If(unsettled > 0):
            dilate_all(nc, A, C, S)
        layer1_first(nc, A, C, S)
        layer1_next(nc, A, C, S, 2)
        layer1_next(nc, A, C, S, 3)
        final(nc, A, C, S)


def setup(nc, A, C):
    with ExitStack() as ctx:
        P = Phase(nc, ctx, "s")
        ch = P.chan("c")
        P.dma("sp", ch, C["W"][:], A["W"])
        P.dma("sp", ch, C["rows"][:], A["rows"].partition_broadcast(128))
        P.dma("sp", ch, C["cols"][:], A["cols"])
        m = P.dma("sp", ch, C["mi"][:], A["mask"])
        a = P.dve(lambda e: e.tensor_copy(C["mf"][:], C["mi"][:]), m)
        P.dve(lambda e: e.tensor_scalar(C["mv"][:], C["mf"][:], 0.0, None, ALU.not_equal), a)
        P.dve(lambda e: e.memset(C["eps"][:], 1e-5))
        P.dve(lambda e: e.memset(C["zero1"][:], 0.0))
        P.dve(lambda e: e.memset(C["flags"][:], 0.0))
        P.dve(lambda e: e.memset(C["onesf"][:], 1.0))
        P.dve(lambda e: e.memset(C["two1"][:], 2.0))
        t = P.sb("t", [128, 3, 128])
        i0 = P.pool(lambda e: e.memset(C["ident"][:], 0.0))
        i1 = P.pool(lambda e: e.affine_select(out=C["ident"][:], in_=C["ident"][:], compare_op=ALU.not_equal,
                                              fill=1.0, base=0, pattern=[[-1, 128]], channel_multiplier=1), i0)
        P.dve(lambda e: e.tensor_copy(C["ident8"][:], C["ident"][:], saturate=False), i1)
        z0 = P.pool(lambda e: e.memset(t[:, 0, :], 0.0))
        z1 = P.pool(lambda e: e.affine_select(out=t[:, 0, :], in_=t[:, 0, :], compare_op=ALU.is_ge,
                                              fill=1.0, base=0, pattern=[[-1, 128]], channel_multiplier=1), z0)
        P.dve(lambda e: e.tensor_copy(C["tri"][:], t[:, 0, :], saturate=False), z1)
        z2 = P.pool(lambda e: e.tensor_tensor(t[:, 1, :], t[:, 0, :], C["ident"][:], ALU.add), z1)
        u = P.dve(lambda e: e.memset(C["U2"][:], 1.0))
        P.dve(lambda e: e.tensor_scalar(C["U2"][:, 0:128], t[:, 1, :], 2.0, None, ALU.mult), z2, u)
        u = P.dve(lambda e: e.memset(C["UL"][:], 2.0))
        P.dve(lambda e: e.tensor_scalar(C["UL"][:, 0:128], t[:, 1, :], 2.0, None, ALU.mult), u)
        w = P.dve(lambda e: e.memset(C["two1"][:, 1:2], 1.0))
        P.dve(lambda e: e.memset(C["zero1"][:, 1:2], 1.0), w)
        P.run()


def col8(t, g):
    return t[:, g * NK:g * NK + NK]


class LayerNorm:

    def __init__(self, P, C):
        self.P, self.C = P, C
        self.st = P.sb("lnst", [128, NK, 6])
        self.mv = P.sb("lnmv", [128, NK, 2])
        self.sd = P.sb("lnsd", [128, NK])
        self.rs = P.sb("lnrs", [128, NK])
        self.last = None

    def __call__(self, x, out, xtok, outfree):
        P = self.P
        a = [P.dve(lambda e, k=k: e.bn_stats(self.st[:, k, :], x[:, k, :]), xtok) for k in range(NK)]
        b = [P.dve(lambda e, k=k: e.bn_aggr(self.mv[:, k, :], self.st[:, k, :]), a[k], self.last) for k in range(NK)]
        s = P.act(lambda e: e.activation(self.sd[:], self.mv[:, :, 1], ACT.Sqrt, bias=self.C["eps"][:, 0:1]), b)
        r = P.dve(lambda e: e.reciprocal(self.rs[:], self.sd[:]), s)
        t = [P.dve(lambda e, k=k: e.tensor_scalar(out[:, k, :], x[:, k, :], self.mv[:, k, 0:1], self.rs[:, k:k + 1],
                                                  ALU.subtract, ALU.mult), r, outfree) for k in range(NK)]
        self.last = t[-1]
        return t[-1]


class RowNorm:

    def __init__(self, P):
        self.P = P
        self.ss = P.sb("rnss", [128, NK])
        self.s2 = P.sb("rns2", [128, NK])
        self.s3 = P.sb("rns3", [128, NK])
        self.rn = P.sb("rnrn", [128, NK])
        self.last = None

    def __call__(self, sq, h, htok, sqfree):
        P = self.P
        a = P.act(lambda e: e.activation(sq[:], h, ACT.Square), htok, sqfree)
        b = P.dve(lambda e: e.tensor_reduce(self.ss[:], sq[:], AXX, ALU.add), a, self.last)
        c = P.dve(lambda e: e.tensor_scalar(self.s2[:], self.ss[:], 1e-24, None, ALU.max), b)
        d = P.act(lambda e: e.activation(self.s3[:], self.s2[:], ACT.Sqrt), c)
        return P.dve(lambda e: e.reciprocal(self.rn[:], self.s3[:]), d), b


def layer0(nc, A, C, S):
    with ExitStack() as ctx:
        P = Phase(nc, ctx, "a")
        adj = [Buf(P.sb(f"adj{i}", [128, NK, N])) for i in range(3)]
        adjch = [P.chan(f"adj{i}") for i in range(3)]
        xt = [Buf(P.sb(f"x{i}", [128, NK, 128])) for i in range(2)]
        xch = [P.chan(f"x{i}") for i in range(2)]
        xsch = P.chan("xs")
        hT = [Buf(P.sb(f"hT{i}", [128, N])) for i in range(2)]
        Hr = [Buf(P.sb(f"Hr{i}", [128, NK, 128])) for i in range(2)]
        nT = [Buf(P.sb(f"nT{i}", [128, N])) for i in range(2)]
        tmp = Buf(P.sb("tmp", [128, NK, 128]))
        ew = [Buf(P.sb(f"ew{i}", [128, 512])) for i in range(3)]
        acc = [Buf(P.ps(f"acc{i}", [128, 512])) for i in range(2)]
        cos = [Buf(P.ps(f"cos{i}", [128, 512])) for i in range(2)]
        pp = Buf(P.ps("pp", [128, NK, 128]))
        ln = LayerNorm(P, C)
        rn = RowNorm(P)
        rnlast = [None]

        units = []
        for u in range(3 * G):
            pi, r = divmod(u, 6)
            units.append((2 * pi + r % 2, r // 2))
        adjtok, xtok = {}, {}

        def load_adj(g):
            b = adj[g % 3]
            adjtok[g] = P.dma("sp", adjch[g % 3], b.t[:], A["adjT"][g].rearrange("(k p) n -> p k n", p=128), b.free)

        def load_x(g, i):
            xtok[g, i] = P.dma("sp", xch[i], flat2(xt[i].t), A["x"][g], xt[i].free)

        def transposes(src, tok):
            for k in range(NK):
                t = P.pe(lambda e, k=k: e.transpose(pp.t[:, k, :], src(k), C["ident"][:]), tok, pp.free,
                         sig=(k == NK - 1))
            return t

        def prep_ln(g):
            t = ln(xt[0].t, tmp.t, xtok[g, 0], tmp.free)
            xt[0].free = [t]
            if g + 1 < G:
                load_x(g + 1, 0)
            def later():
                tt = transposes(lambda k: tmp.t[:, k, :], t)
                tmp.free = [tt]
                h = hT[g % 2]
                ev = P.act(lambda e: e.activation(h.t[:], pp.t[:].rearrange("p k d -> p (k d)"), ACT.Relu), tt, h.free)
                pp.free = [ev]
                h.ready = ev
            return later

        def prep_h(u):
            g, i = units[u]
            h, H, n = hT[g % 2], Hr[g % 2], nT[g % 2]
            for k in range(NK):
                t = P.pe(lambda e, k=k: e.matmul(pp.t[:, k, :], h.t[:, blk(k)], C["W"][:, i, :], start=True, stop=True),
                         h.ready, pp.free, sig=(k == NK - 1))
            h.free = [t]
            H.ready = P.dve(lambda e: e.tensor_tensor(
                H.t[:], pp.t[:], C["rows"][:, i, :].unsqueeze(1).to_broadcast([128, NK, 128]), ALU.add), t, H.free)
            pp.free = [H.ready]
            r, b = rn(tmp.t, H.t[:], H.ready, tmp.free)
            m = P.dve(lambda e: e.tensor_tensor(tmp.t[:], H.t[:], bc(rn.rn[:], 128), ALU.mult), r, H.ready, b)
            rn.last = m

            def later():
                tt = transposes(lambda k: tmp.t[:, k, :], m)
                tmp.free = [tt]
                n.ready = P.act(lambda e: e.activation(n.t[:], pp.t[:].rearrange("p k d -> p (k d)"), ACT.Copy),
                                tt, n.free)
                pp.free = [n.ready]
            return later

        def evac(u):
            g, i = units[u]
            h = hT[g % 2]
            f = ACT.Relu if i < 2 else ACT.Copy
            for j in range(2):
                t = P.act(lambda e, j=j: e.activation(h.t[:, j * 512:j * 512 + 512], acc[j].t[:], f),
                          acc[j].ready, h.free)
                acc[j].free = [t]
            h.ready = t

        def post(u):
            g, i = units[u]
            h, x = hT[g % 2], xt[1]
            tt = transposes(lambda k: h.t[:, blk(k)], h.ready)
            h.free = [tt]
            s = P.dve(lambda e: e.tensor_tensor(x.t[:], pp.t[:], x.t[:], ALU.add), tt, xtok[g, 1])
            pp.free = [s]
            x.free = [P.dma("act", xsch, S["x1"][g], flat2(x.t), s)]
            if g + 1 < G:
                load_x(g + 1, 1)

        dil = Dilation(P, C)

        for g in range(3):
            if g < 2:
                load_x(0, g)
            load_adj(g)
        prep_ln(0)()
        prep_h(0)()
        dil.bits(0, adj[0].t, adjtok[0])
        dil.bits(1, adj[1].t, adjtok[1])
        micro = dil.steps(0, A, S)

        hooks = {}

        def at(u, k, fn):
            hooks.setdefault((u, k), []).append(fn)

        steps = [(u, k) for u in range(3 * G) for k in range(NK)]
        later = {}

        def do_cos(u, k, j):
            g, i = units[u]
            n, a, c = nT[g % 2], adj[g % 3], cos[j]
            t = P.pe(lambda e: e.matmul(c.t[:], n.t[:, blk(k)], n.t[:, j * 512:j * 512 + 512], start=True, stop=True),
                     n.ready, c.free)
            w = ew[(2 * (u * NK + k) + j) % 3]
            m = P.dve(lambda e: e.tensor_tensor(w.t[:], a.t[:, k, j * 512:j * 512 + 512], c.t[:], ALU.mult),
                      t, w.free, adjtok[g])
            c.free = [m]
            w.ready = m
            if k == NK - 1 and j == 1:
                n.free = [t]
                if i == 2:
                    a.free = [m, dil.bitsdone.get(g)]
                    if g + 3 < G:
                        load_adj(g + 3)

        def do_agg(u, k, j):
            g, i = units[u]
            H, w = Hr[g % 2], ew[(2 * (u * NK + k) + j) % 3]
            t = P.pe(lambda e: e.matmul(acc[j].t[:], H.t[:, k, :], w.t[:], start=(k == 0), stop=(k == NK - 1)),
                     w.ready, H.ready, acc[j].free if k == 0 else None)
            w.free = [t]
            acc[j].ready = t
            if k == NK - 1 and j == 1:
                H.free = [t]

        do_cos(0, 0, 0)
        do_cos(0, 0, 1)
        done = 0
        for s, (u, k) in enumerate(steps):
            pi, r = divmod(u, 6)
            pos = r * NK + k
            if k == 1 and u >= 1 and units[u - 1][1] == 2:
                post(u - 1)
            if u + 1 < 3 * G:
                g2, i2 = units[u + 1]
                if i2 == 0:
                    if k == 0:
                        later["ln"] = prep_ln(g2)
                    if k == 2:
                        later["ln"]()
                    if k == 3:
                        later["h"] = prep_h(u + 1)
                    if k == 6:
                        later["h"]()
                else:
                    if k == 1:
                        later["h"] = prep_h(u + 1)
                    if k == 4:
                        later["h"]()
            for j in range(2):
                if s + 1 < len(steps):
                    do_cos(*steps[s + 1], j)
                do_agg(u, k, j)
            if k == NK - 1:
                evac(u)
            while done * 6 * NK < (pos + 1) * len(micro):
                if done >= len(micro):
                    break
                micro[done]()
                done += 1
            if pos == 6 * NK - 1 and pi + 1 < G // 2:
                for g in (2 * pi + 2, 2 * pi + 3):
                    dil.bits(g, adj[g % 3].t, adjtok[g])
                micro = dil.steps(pi + 1, A, S)
                done = 0
        post(3 * G - 1)
        P.run()


class Dilation:

    def __init__(self, P, C):
        self.C = C
        self.AT = [Buf(P.sb(f"AT{i}", [128, NK, N], FP8)) for i in range(2)]
        self.R = [Buf(P.sb(f"R{i}", [128, NK, N], FP8)) for i in range(2)]
        self.af = [Buf(P.sb(f"af{i}", [128, 512])) for i in range(2)]
        self.Ab = [Buf(P.sb(f"Ab{i}", [128, N], BF16)) for i in range(4)]
        self.Au = [P.sb(f"Au{i}", [128, 128], BF16) for i in range(2)]
        self.Sd = [Buf(P.sb(f"Sd{i}", [128, 128], FP8)) for i in range(2)]
        self.Ru = [[P.sb(f"Ru{i}{j}", [128, 128], FP8) for j in range(2)] for i in range(2)]
        self.v8 = P.sb("v8", [128, 128], BF16)
        self.base = P.sb("base", [128, 2, 2])
        self.v = [Buf(P.sb(f"v{i}", [128, 512], F16)) for i in range(2)]
        self.kp = [Buf(P.sb(f"kp{i}", [128, N], U8)) for i in range(2)]
        self.cnt = P.sb("cnt", [128, 2])
        self.small = {n: P.sb(f"sm_{n}", [128, 2]) for n in ("t", "sf", "sc", "va", "h", "b", "c", "b2")}
        self.rank = Buf(P.ps("rank", [128, 2, 144]))
        self.wide = Buf(P.ps("wide", [128, 512]))
        self.attach(P)

    def attach(self, P):
        self.P = P
        self.afch = [P.chan(f"af{i}") for i in range(2)]
        self.kpch = [P.chan(f"kp{i}") for i in range(2)]
        for b in (*self.AT, *self.R, *self.af, *self.Ab, *self.Sd, *self.v, *self.kp, self.rank, self.wide):
            b.free, b.ready = [], None
        self.bitsdone = {}
        self.nv = self.nk = 0
        self.smallfree = []
        self.basetok = self.v8tok = None
        self.autok, self.rtok, self.lowtok, self.prev = [None] * 2, [None] * 2, [None] * 2, [None] * 2
        self.ruletok = None

    def bits(self, g, adj, tok):
        b = self.AT[g % 2]
        for k in range(NK):
            t = self.P.pool(lambda e, k=k: e.tensor_scalar(b.t[:, k, :].bitcast(U8), adj[:, k, :], 0.0, ONE8, ALU.is_gt, ALU.mult),
                            tok, b.free)
        self.bitsdone[g] = t
        b.ready = t

    def rowbits(self, i, k, src):
        b = self.Ab[2 * (k % 2) + i]
        for j in range(2):
            a = self.af[j]
            h = slice(j * 512, j * 512 + 512)
            l = self.P.dma("sp", self.afch[j], a.t[:], src[:, h], a.free)
            b.ready = self.P.pool(lambda e, a=a, h=h: e.tensor_scalar(b.t[:, h], a.t[:], 0.0, None, ALU.is_gt), l, b.free)
            a.free = [b.ready]

    def begin(self, i, k):
        P, C = self.P, self.C
        AT, R, ab = self.AT[i], self.R[i], self.Ab[2 * (k % 2) + i]
        low = AT.ready
        if k:
            low = P.dve(lambda e: e.tensor_tensor(AT.t[:, 0:k, blk(k)], AT.t[:, 0:k, blk(k)], R.t[:, 0:k, blk(k)],
                                                  ALU.is_gt, saturate=False), AT.ready, R.ready)
        others = [q for q in range(NK) if q != k]
        for q in others:
            t = P.pe(lambda e, q=q: e.matmul(self.rank.t[:, i, 132:134], AT.t[:, q, blk(k)],
                                             (C["two1"] if q < k else C["zero1"])[:], start=(q == others[0]),
                                             stop=(q == others[-1])),
                     low, AT.ready, self.rank.free, sig=(q == others[-1]))
        au = P.dve(lambda e: e.tensor_tensor(self.Au[i][:], ab.t[:, blk(k)], C["tri"][:], ALU.mult), ab.ready)
        z = P.dve(lambda e: e.memset(self.Ru[i][1][:], 0.0))
        self.autok[i], self.rtok[i], self.lowtok[i] = au, z, low
        return t

    def rule(self, w, mv):
        P, C, s = self.P, self.C, self.small
        num, sf = self.cnt, s["sf"]
        n = P.dve(lambda e: e.tensor_tensor(num[:], self.rank.t[:, :, 128], self.base[:, :, 1], ALU.add), w, self.basetok)
        a = P.dve(lambda e: e.tensor_scalar(s["t"][:], num[:], 0.5, 0.5, ALU.add, ALU.mult), n)
        c = P.dve(lambda e: e.scalar_tensor_tensor(s["sc"][:], num[:], 10.5, mv, ALU.is_gt, ALU.mult), n, self.smallfree)
        d = P.dve(lambda e: e.scalar_tensor_tensor(s["va"][:], num[:], 1.5, mv, ALU.is_gt, ALU.mult), n)
        b = P.dve(lambda e: e.tensor_scalar(sf[:], s["t"][:], MAGIC, MAGIC, ALU.add, ALU.subtract), a, self.smallfree)
        h = P.dve(lambda e: e.scalar_tensor_tensor(s["h"][:], s["sc"][:], -4.0, s["va"][:], ALU.mult, ALU.add), c, d)
        p = P.dve(lambda e: e.tensor_tensor(s["b"][:], sf[:], s["h"][:], ALU.mult), h, b, self.smallfree)
        q = P.dve(lambda e: e.tensor_tensor(s["c"][:], s["sc"][:], self.base[:, :, 0], ALU.mult), c)
        b2 = P.dve(lambda e: e.tensor_tensor(s["b2"][:], s["b"][:], s["c"][:], ALU.add), p, q, self.smallfree)
        self.smallfree = []
        self.ruletok = [b2, p]

    def round(self, mv, r, last, first):
        P, C, s = self.P, self.C, self.small
        w = []
        for i in range(2):
            src = self.AT[i].t[:, self.k, blk(self.k)] if first else self.Sd[i].t[:]
            t = P.pe(lambda e, i=i, src=src: e.matmul(self.rank.t[:, i, 0:129], src, C["U2"][:, 0:129], start=True, stop=True),
                     self.lowtok[i] if first else self.Sd[i].ready, self.rank.free, self.basetok)
            self.Sd[i].free = [t]
            w.append(t)
        self.rule(w, mv)
        free = []
        for i in range(2):
            v = self.v[self.nv % 2]
            self.nv += 1
            a = P.act(lambda e, i=i, v=v: e.activation(v.t[:, 0:128], self.rank.t[:, i, 0:128], ACT.Abs,
                                                       bias=s["b2"][:, i:i + 1], scale=s["sc"][:, i:i + 1]),
                      w, self.ruletok, v.free)
            free.append(a)
            out = self.Ru[i][r % 2]
            x = P.dve(lambda e, i=i, v=v, out=out: e.scalar_tensor_tensor(
                out[:], v.t[:, 0:128], s["sf"][:, i:i + 1], self.Au[i][:], ALU.is_equal, ALU.mult, saturate=False),
                a, self.autok[i])
            v.free = [x]
            self.prev[i], self.rtok[i] = self.rtok[i], x
            if not last:
                at = self.AT[i].t[:, self.k, blk(self.k)]
                self.Sd[i].ready = P.dve(lambda e, i=i, out=out, at=at: e.tensor_tensor(
                    self.Sd[i].t[:], at, out[:], ALU.is_gt, saturate=False), x, self.Sd[i].free)
        self.rank.free = free
        self.smallfree = free + [x]

    def settled(self, i, col):
        self.v8tok = self.P.dve(lambda e: e.scalar_tensor_tensor(
            self.v8[:], self.Ru[i][0][:], 1.0, self.Ru[i][1][:], ALU.mult, ALU.not_equal, accum_out=col),
            self.rtok[i], self.prev[i], self.v8tok)

    def full(self, i):
        P, C, s, k = self.P, self.C, self.small, self.k
        AT, R, ab = self.AT[i], self.R[i], self.Ab[2 * (k % 2) + i]
        out = []
        for j in range(2):
            qs = [q for q in range(NK) if q * 128 < j * 512 + 512]
            for q in qs:
                lo = max(q * 128, j * 512)
                src = self.Sd[i].t[:] if q == k else AT.t[:, q, blk(k)]
                t = P.pe(lambda e, q=q, lo=lo, src=src, j=j: e.matmul(
                    self.wide.t[:, lo - j * 512:512], src, C["UL"][:, lo - q * 128:j * 512 + 512 - q * 128],
                    start=(q == 0), stop=(q == qs[-1]), skip_group_check=True),
                    self.wide.free, self.Sd[i].ready, self.lowtok[i], AT.ready, sig=(q == qs[-1]))
            v = self.v[self.nv % 2]
            self.nv += 1
            a = P.act(lambda e, v=v: e.activation(v.t[:], self.wide.t[:], ACT.Abs, bias=s["b"][:, i:i + 1],
                                                  scale=s["sc"][:, i:i + 1]), t, self.ruletok, v.free)
            self.wide.free = [a]
            x = P.dve(lambda e, v=v, j=j: e.scalar_tensor_tensor(
                R.t[:, k, j * 512:j * 512 + 512], v.t[:], s["sf"][:, i:i + 1], ab.t[:, j * 512:j * 512 + 512],
                ALU.is_equal, ALU.mult, saturate=False), a, ab.ready, R.free)
            v.free = [x]
            out += [a, x]
        self.Sd[i].free = [t]
        AT.free = [t]
        ab.free = [x, self.autok[i]]
        R.ready = x
        self.smallfree = self.smallfree + out

    def mask(self, i, q, dst):
        P, C = self.P, self.C
        R = self.R[i]
        kp = self.kp[self.nk % 2]
        ch = self.kpch[self.nk % 2]
        self.nk += 1
        for j in range(2):
            P.pe(lambda e, j=j: e.matmul(self.wide.t[:], C["ident8"][:], R.t[:, q, j * 512:j * 512 + 512],
                                         start=True, stop=False, skip_group_check=True), R.ready, self.wide.free, sig=False)
            for b in range(4):
                t = P.pe(lambda e, j=j, b=b: e.matmul(self.wide.t[:, blk(b)], R.t[:, 4 * j + b, blk(q)], C["ident8"][:],
                                                      start=False, stop=(b == 3), skip_group_check=True), sig=(b == 3))
            a = P.act(lambda e, j=j: e.activation(kp.t[:, j * 512:j * 512 + 512], self.wide.t[:], ACT.Relu,
                                                  bias=1.0, scale=-1.0), t, kp.free)
            self.wide.free = [a]
        if q == NK - 1:
            R.free = [t]
        st = P.dma("sp", ch, dst, kp.t[:], a)
        kp.free = [st]

    def start(self, k):
        self.k = k
        t = [self.begin(i, k) for i in range(2)]
        self.basetok = self.P.dve(lambda e: e.tensor_copy(self.base[:], self.rank.t[:, :, 132:134]), t, self.smallfree)
        self.rank.free = [self.basetok]

    def steps(self, pi, A, S):
        C, out = self.C, []
        mv = C["mv"][:].rearrange("p (g k) -> p g k", k=NK)[:, 2 * pi:2 * pi + 2, :]

        def rows(k):
            for i in range(2):
                self.rowbits(i, k, A["adj"][2 * pi + i, blk(k), :])

        def start(k):
            if k == 0:
                rows(0)
            self.start(k)
            if k + 1 < NK:
                rows(k + 1)

        def full(k, i):
            c = (2 * pi + i) * NK + k
            self.settled(i, C["flags"][:, c:c + 1])
            self.full(i)

        for k in range(NK):
            for r in range(ROUNDS[k]):
                out.append(lambda k=k, r=r: (start(k) if r == 0 else None,
                                             self.round(mv[:, :, k], r, r == ROUNDS[k] - 1, r == 0)))
            out.append(lambda k=k: full(k, 0))
            out.append(lambda k=k: full(k, 1))
        for i in range(2):
            for q in range(NK):
                out.append(lambda i=i, q=q: self.mask(i, q, S["keep"][2 * pi + i, q]))
        return out


def changed(nc, C):
    with ExitStack() as ctx:
        P = Phase(nc, ctx, "n")
        r, ps = P.sb("r", [128, 1]), P.ps("ps", [128, 1])
        a = P.dve(lambda e: e.tensor_reduce(r[:], C["flags"][:], AXX, ALU.add))
        b = P.pe(lambda e: e.matmul(ps[:], C["onesf"][:], r[:], start=True, stop=True), a)
        P.dve(lambda e: e.tensor_copy(C["flag"][:], ps[:]), b)
        P.run()
    return nc.values_load(C["flag"][0:1, 0:1], min_val=0, max_val=128 * 128 * 128)


def dilate_all(nc, A, C, S):
    with ExitStack() as ctx:
        M = Phase(nc, ctx, "g")
        adj = M.sb("adj", [128, NK, N])
        mi, mf, mv = M.sb("mi", [128, 2, NK], I32), M.sb("mf", [128, 2, NK]), M.sb("mv", [128, 2, NK])
        dil = Dilation(M, C)

        def stage(fill):
            P = Phase(nc, ctx, "g", M.sems)
            dil.attach(P)
            fill(P)
            P.run()
            for s in P.sems.values():
                nc.sync.sem_clear(s)
            nc.all_engine_barrier()

        M.chan("l"), M.chan("m")
        with nc.Fori(0, G // 2) as pair:
            def load(i):
                def fill(P):
                    g = pair * 2 + i
                    t = P.dma("sp", P.chan("l"), adj[:],
                              A["adjT"][bass.ds(g, 1)].rearrange("o (k p) n -> p (o k) n", p=128))
                    dil.bits(i, adj, t)
                    t = P.dma("sp", P.chan("m"), mi[:, i, :], A["mask"][:, bass.ds(g * NK, NK)])
                    a = P.dve(lambda e: e.tensor_copy(mf[:, i, :], mi[:, i, :]), t)
                    P.dve(lambda e: e.tensor_scalar(mv[:, i, :], mf[:, i, :], 0.0, None, ALU.not_equal), a)
                return fill

            def start(k):
                def fill(P):
                    for i in range(2):
                        src = A["adj"][bass.ds(pair * 2 + i, 1)].rearrange("o n m -> (o n) m")
                        dil.rowbits(i, k, src[blk(k), :])
                    dil.start(k)
                    for i in range(2):
                        P.dve(lambda e, i=i: e.tensor_copy(dil.Sd[i].t[:], dil.AT[i].t[:, k, blk(k)], saturate=False))
                return fill

            def masks(i, q):
                def fill(P):
                    dil.mask(i, q, S["keep"][bass.ds(pair * 2 + i, 1), q].rearrange("o p n -> (o p) n"))
                return fill

            stage(load(0))
            stage(load(1))
            for k in range(NK):
                stage(start(k))
                with nc.Fori(0, 128):
                    stage(lambda P: dil.round(mv[:, :, k], 0, False, False))
                stage(lambda P: (dil.full(0), dil.full(1)))
            for i in range(2):
                for q in range(NK):
                    stage(masks(i, q))


class Sage:

    def __init__(self, P, A, C, S, adjs):
        self.P, self.A, self.C, self.S = P, A, C, S
        self.adj = [Buf(P.sb(f"adj{i}", [128, NK, N])) for i in range(adjs)]
        self.adjch = [P.chan(f"adj{i}") for i in range(adjs)]
        self.kp = [Buf(P.sb(f"kp{i}", [128, NK, N], U8)) for i in range(2)]
        self.kpch = [P.chan(f"kp{i}") for i in range(2)]
        self.acc = [Buf(P.ps(f"acc{i}", [128, 512])) for i in range(2)]
        self.masked = {}
        self.ltok = {}

    def load(self, g):
        P, n = self.P, len(self.adj)
        b, c = self.adj[g % n], self.kp[g % 2]
        a = P.dma("sp", self.adjch[g % n], b.t[:], self.A["adjT"][g].rearrange("(k p) n -> p k n", p=128), b.free)
        m = P.dma("sp", self.kpch[g % 2], c.t[:], self.S["keep"][g].rearrange("k p n -> p k n"), c.free)
        self.ltok[g] = [a, m]

    def mask(self, g):
        P, n = self.P, len(self.adj)
        b, c = self.adj[g % n], self.kp[g % 2]
        self.masked[g] = [P.dve(lambda e, q=q: e.tensor_tensor(b.t[:, q, :], b.t[:, q, :], c.t[:, q, :], ALU.mult),
                                self.ltok[g]) for q in range(NK)]
        c.free = [self.masked[g][-1]]

    def agg(self, g, rows, tok):
        P, b = self.P, self.adj[g % len(self.adj)]
        for q in range(NK):
            for j in range(2):
                t = P.pe(lambda e, q=q, j=j: e.matmul(self.acc[j].t[:], rows[:, q, :], b.t[:, q, j * 512:j * 512 + 512],
                                                      start=(q == 0), stop=(q == NK - 1)),
                         tok, self.masked[g][q], self.acc[j].free if q == 0 else None, sig=(q == NK - 1))
                self.acc[j].ready = t
        return t

    def evac(self, dst, free):
        P = self.P
        for j in range(2):
            t = P.act(lambda e, j=j: e.activation(dst[:, j * 512:j * 512 + 512], self.acc[j].t[:], ACT.Copy),
                      self.acc[j].ready, free)
            self.acc[j].free = [t]
        return t


def flat2(t):
    return t[:].rearrange("p k d -> p (k d)")


class Dense:

    def __init__(self, P, C):
        self.P, self.C = P, C
        self.p1 = Buf(P.ps("p1", [128, NK, 128]))
        self.p2 = Buf(P.ps("p2", [128, NK, 128]))
        self.o = Buf(P.sb("o", [128, NK, 128]))
        self.sq = Buf(P.sb("sq", [128, NK, 128]))
        self.z = [Buf(P.sb(f"z{i}", [128, NK, 128])) for i in range(2)]
        self.zT = [Buf(P.sb(f"zT{i}", [128, N])) for i in range(2)]
        self.rn = RowNorm(P)
        self.rm = P.sb("rm", [128, NK])

    def mm(self, dst, lhsT, rhs, *waits):
        P = self.P
        for k in range(NK):
            t = P.pe(lambda e, k=k: e.matmul(dst.t[:, k, :], lhsT[:, blk(k)], rhs, start=True, stop=True),
                     waits, dst.free, sig=(k == NK - 1))
        return t

    def __call__(self, g, aggT, hT, Wr, Wx, bias, stats, waits, rank1=None):
        P, C, o = self.P, self.C, self.o
        z, zT = self.z[g % 2], self.zT[g % 2]
        a = self.mm(self.p1, aggT, Wr, waits)
        b = self.mm(self.p2, hT, Wx, waits)
        c = P.dve(lambda e: e.tensor_tensor(o.t[:], self.p2.t[:], bias.unsqueeze(1).to_broadcast([128, NK, 128]),
                                            ALU.add), b, o.free)
        self.p2.free = [c]
        for k in range(NK):
            f = P.dve(lambda e, k=k: e.scalar_tensor_tensor(o.t[:, k, :], self.p1.t[:, k, :], C["rdeg"][:, g, k:k + 1],
                                                            o.t[:, k, :], ALU.mult, ALU.add), a, c)
        self.p1.free = [f]
        if rank1 is not None:
            f0 = f
            for k in range(NK):
                f = P.dve(lambda e, k=k: e.scalar_tensor_tensor(o.t[:, k, :], rank1, C["rho"][:, g, k:k + 1],
                                                                o.t[:, k, :], ALU.mult, ALU.add), f0)
        r, ss = self.rn(self.sq.t, o.t[:], f, self.sq.free)
        self.sq.free = [ss]
        m = P.dve(lambda e: e.tensor_tensor(self.rm[:], self.rn.rn[:], col8(C["mf"], g), ALU.mult), r)
        s = P.dve(lambda e: e.tensor_tensor(o.t[:], o.t[:], bc(self.rm[:], 128), ALU.mult), m, ss)
        self.rn.last = s
        z.ready = P.act(lambda e: e.activation(z.t[:], o.t[:], ACT.Relu), s, z.free)
        o.free = [z.ready]
        z.free = []

        def later():
            for k in range(NK):
                t = P.pe(lambda e, k=k: e.transpose(self.p2.t[:, k, :], z.t[:, k, :], C["ident"][:]), z.ready,
                         self.p2.free, sig=(k == NK - 1))
            z.free.append(t)
            zT.ready = P.act(lambda e: e.activation(zT.t[:], flat2(self.p2.t), ACT.Copy), t, zT.free)
            self.p2.free = [zT.ready]
            st = [P.dve(lambda e, j=j: e.bn_stats(stats[:, 2 * g + j, :], zT.t[:, j * 512:j * 512 + 512]), zT.ready)
                  for j in range(2)]
            return st
        return (a, b), later


def layer1_first(nc, A, C, S):
    with ExitStack() as ctx:
        P = Phase(nc, ctx, "b")
        sg = Sage(P, A, C, S, 3)
        dn = Dense(P, C)
        ln = LayerNorm(P, C)
        stats = nc_stats(P, C)
        x = [Buf(P.sb(f"x{i}", [128, NK, 128])) for i in range(2)]
        xch = [P.chan(f"x{i}") for i in range(2)]
        h = [Buf(P.sb(f"h{i}", [128, NK, 128])) for i in range(2)]
        hT = [Buf(P.sb(f"hT{i}", [128, N])) for i in range(2)]
        aT = Buf(P.sb("aT", [128, N]))
        a1 = Buf(P.sb("a1", [128, N]))
        a1ch = P.chan("a1")
        zch = [P.chan(f"z{i}") for i in range(2)]
        dsum = Buf(P.sb("dsum", [128, N]))
        dg = P.sb("dg", [128, NK])
        dp = P.ps("dp", [128, NK])
        pt = dn.p1
        xtok = {}

        def load(g):
            sg.load(g)
            xtok[g] = P.dma("sp", xch[g % 2], flat2(x[g % 2].t), S["x1"][g], x[g % 2].free)

        def prep(g):
            sg.mask(g)
            hb, hTb = h[g % 2], hT[g % 2]
            t = ln(x[g % 2].t, x[g % 2].t, xtok[g], None)
            hb.ready = P.act(lambda e: e.activation(hb.t[:], x[g % 2].t[:], ACT.Relu), t, hb.free)
            x[g % 2].free = [hb.ready]
            b = sg.adj[g % 3]
            m = sg.masked[g]
            d = P.pool(lambda e: e.tensor_tensor(dsum.t[:], b.t[:, 0, :], b.t[:, 1, :], ALU.add), m[0], m[1], dsum.free)
            for q in range(2, NK):
                d = P.pool(lambda e, q=q: e.tensor_tensor(dsum.t[:], dsum.t[:], b.t[:, q, :], ALU.add), d, m[q])
            b.pool = d
            dsum.ready = d

        def prep2(g):
            hb, hTb = h[g % 2], hT[g % 2]
            for k in range(NK):
                t = P.pe(lambda e, k=k: e.transpose(pt.t[:, k, :], hb.t[:, k, :], C["ident"][:]), hb.ready, pt.free,
                         sig=(k == NK - 1))
            hb.free = [t]
            hTb.ready = P.act(lambda e: e.activation(hTb.t[:], flat2(pt.t), ACT.Copy), t, hTb.free)
            pt.free = [hTb.ready]

        def degree(g):
            for k in range(NK):
                t = P.pe(lambda e, k=k: e.matmul(dp[:, k:k + 1], dsum.t[:, blk(k)], C["onesf"][:, 0:1], start=True,
                                                 stop=True), dsum.ready, degfree, sig=(k == NK - 1))
            dsum.free = [t]
            a = P.dve(lambda e: e.tensor_scalar(dg[:], dp[:], 1.0, None, ALU.max), t, degfree)
            b = P.dve(lambda e: e.reciprocal(C["rdeg"][:, g, :], dg[:]), a)
            c = P.dve(lambda e: e.tensor_tensor(C["rho"][:, g, :], dp[:], C["rdeg"][:, g, :], ALU.mult), b)
            degfree[:] = [b, c]
            return b

        degfree = []
        state = {}

        def first(g):
            t = sg.agg(g, h[g % 2].t, h[g % 2].ready)
            h[g % 2].free.append(t)
            dt = degree(g)
            aT.ready = sg.evac(aT.t, aT.free)
            (a, b), later = dn(g, aT.t, hT[g % 2].t, C["W"][:, 3, :], C["W"][:, 4, :], C["rows"][:, 3, :], stats,
                               [aT.ready, hT[g % 2].ready, dt])
            aT.free = [a]
            hT[g % 2].free = [b]
            state[g] = later

        def second(g):
            st = state[g]()
            z, zT = dn.z[g % 2], dn.zT[g % 2]
            zs = P.dma("act", zch[g % 2], S["z1"][g], zT.t[:], zT.ready)
            zT.free = [zs] + st
            t = sg.agg(g, z.t, z.ready)
            z.free.append(t)
            b = sg.adj[g % 3]
            b.free = [t, b.pool]
            e = sg.evac(a1.t, a1.free)
            a1.free = [P.dma("act", a1ch, S["ag1"][g], a1.t[:], e)]
            if g + 3 < G:
                load(g + 3)

        load(0)
        load(1)
        prep(0)
        prep2(0)
        load(2)
        for g in range(G):
            first(g)
            if g + 1 < G:
                prep(g + 1)
                prep2(g + 1)
            if g:
                second(g - 1)
        second(G - 1)
        fold(P, C, stats, 1, st_all(P, dn))
        P.run()


def nc_stats(P, C):
    return P.sb("stats", [128, 2 * G, 6])


def st_all(P, dn):
    return [(P.lanes["dve"].sem, P.lanes["dve"].count)]


def fold(P, C, stats, l, waits):
    ag = P.sb("ag", [128, 2])
    sd = P.sb("bsd", [128, 1])
    rs = P.sb("brs", [128, 1])
    s = P.sb("bs", [128, 1])
    ms = P.sb("bms", [128, 1])
    t = P.sb("bt", [128, 1])
    tb = P.sb("btb", [128, 128])
    pv = P.ps("pv", [128, 128])
    a = P.dve(lambda e: e.bn_aggr(ag[:], stats[:].rearrange("p a b -> p (a b)")), waits)
    b = P.act(lambda e: e.activation(sd[:], ag[:, 1:2], ACT.Sqrt, bias=C["eps"][:, 0:1]), a)
    c = P.dve(lambda e: e.reciprocal(rs[:], sd[:]), b)
    d = P.dve(lambda e: e.tensor_tensor(s[:], rs[:], C["cols"][:, 2 * (l - 1):2 * l - 1], ALU.mult), c)
    f = P.dve(lambda e: e.tensor_tensor(ms[:], ag[:, 0:1], s[:], ALU.mult), d)
    h = P.dve(lambda e: e.tensor_tensor(t[:], C["cols"][:, 2 * l - 1:2 * l], ms[:], ALU.subtract), f)
    k = P.dve(lambda e: e.tensor_scalar(tb[:], C["onesf"][:], t[:, 0:1], None, ALU.mult), h)
    use = [(8 + l, 9 + l)] if l == 3 else [(3 + 2 * l, 6), (4 + 2 * l, 3 + l), (8 + l, 9 + l)]
    free = None
    for w, row in use:
        m = P.pe(lambda e, w=w: e.matmul(pv[:], tb[:], C["W"][:, w, :], start=True, stop=True), k, free)
        if row == 6:
            free = P.dve(lambda e: e.tensor_copy(C["rows"][:, 6, :], pv[:]), m)
        else:
            free = P.dve(lambda e, row=row: e.tensor_tensor(C["rows"][:, row, :], C["rows"][:, row, :], pv[:], ALU.add), m)
        P.dve(lambda e, w=w: e.tensor_scalar(C["W"][:, w, :], C["W"][:, w, :], s[:, 0:1], None, ALU.mult), m, d)


def layer1_next(nc, A, C, S, l):
    with ExitStack() as ctx:
        P = Phase(nc, ctx, f"c{l}")
        sums = l == 2
        sg = Sage(P, A, C, S, 3) if sums else None
        dn = Dense(P, C)
        stats = nc_stats(P, C)
        zi = [Buf(P.sb(f"zi{i}", [128, N])) for i in range(3)]
        zich = [P.chan(f"zi{i}") for i in range(3)]
        ai = [Buf(P.sb(f"ai{i}", [128, N])) for i in range(3)]
        aich = [P.chan(f"ai{i}") for i in range(3)]
        zch = [P.chan(f"z{i}") for i in range(2)]
        y = Buf(P.sb("y", [128, NK, 128]))
        yi = [Buf(P.sb(f"yi{i}", [128, NK, 128])) for i in range(3)]
        yich = [P.chan(f"yi{i}") for i in range(3)]
        ych = P.chan("y")
        a2 = Buf(P.sb("a2", [128, N]))
        a2ch = P.chan("a2")
        tok, state = {}, {}
        zsrc, asrc, zdst = S[f"z{l - 1}"], S[f"ag{l - 1}"], S[f"z{l}"]

        def load(g):
            i = g % 3
            tok[g] = [P.dma("sp", zich[i], zi[i].t[:], zsrc[g], zi[i].free),
                      P.dma("sp", aich[i], ai[i].t[:], asrc[g], ai[i].free)]
            if not sums:
                tok[g].append(P.dma("sp", yich[i], flat2(yi[i].t), S["ya"][g], yi[i].free))
            if sums:
                sg.load(g)

        def first(g):
            i = g % 3
            (a, b), later = dn(g, ai[i].t, zi[i].t, C["W"][:, 1 + 2 * l, :], C["W"][:, 2 + 2 * l, :], C["rows"][:, 2 + l, :],
                               stats, tok[g], rank1=C["rows"][:, 6, :])
            ai[i].free = [a]
            zi[i].free = [b]
            state[g] = later
            if sums:
                sg.mask(g)

        def wl(g):
            i = g % 3
            m = dn.mm(dn.p1, zi[i].t, C["W"][:, 7 + l, :], tok[g])
            zi[i].free = zi[i].free + [m]
            if l == 2:
                e = P.act(lambda e: e.activation(y.t[:], dn.p1.t[:], ACT.Copy), m, y.free)
            else:
                e = P.dve(lambda e: e.tensor_tensor(y.t[:], dn.p1.t[:], yi[i].t[:], ALU.add), m, y.free, tok[g])
                yi[i].free = [e]
            dn.p1.free = [e]
            y.free = [P.dma("act", ych, S["ya" if l == 2 else "yb"][g], flat2(y.t), e)]

        def second(g):
            st = state[g]()
            z, zT = dn.z[g % 2], dn.zT[g % 2]
            zs = P.dma("act", zch[g % 2], zdst[g], zT.t[:], zT.ready)
            zT.free = [zs] + st
            if sums:
                t = sg.agg(g, z.t, z.ready)
                z.free.append(t)
                sg.adj[g % 3].free = [t]
                e = sg.evac(a2.t, a2.free)
                a2.free = [P.dma("act", a2ch, S["ag2"][g], a2.t[:], e)]

        load(0)
        load(1)
        for g in range(G):
            first(g)
            if g:
                second(g - 1)
            if g + 2 < G:
                load(g + 2)
            wl(g)
        second(G - 1)
        fold(P, C, stats, l, st_all(P, dn))
        P.run()


def final(nc, A, C, S):
    with ExitStack() as ctx:
        P = Phase(nc, ctx, "f")
        tr = P.sb("tr", [128, 128])
        u = P.dve(lambda e: e.tensor_tensor(tr[:], C["rows"][:, 10, :], C["rows"][:, 11, :], ALU.add))
        u = P.dve(lambda e: e.tensor_tensor(tr[:], tr[:], C["rows"][:, 12, :], ALU.add), u)
        nb = 3
        zi = [Buf(P.sb(f"zi{i}", [128, N])) for i in range(nb)]
        yi = [Buf(P.sb(f"yi{i}", [128, NK, 128])) for i in range(nb)]
        xi = [Buf(P.sb(f"xi{i}", [128, NK, 128])) for i in range(nb)]
        zch = [P.chan(f"zi{i}") for i in range(nb)]
        ych = [P.chan(f"yi{i}") for i in range(nb)]
        xch = [P.chan(f"xi{i}") for i in range(nb)]
        och = [P.chan(f"o{i}") for i in range(nb)]
        pp = [Buf(P.ps(f"p{i}", [128, NK, 128])) for i in range(2)]
        for g in range(G):
            i = g % nb
            p = pp[g % 2]
            lz = P.dma("sp", zch[i], zi[i].t[:], S["z3"][g], zi[i].free)
            ly = P.dma("sp", ych[i], flat2(yi[i].t), S["yb"][g], yi[i].free)
            lx = P.dma("sp", xch[i], flat2(xi[i].t), S["x1"][g], xi[i].free)
            for k in range(NK):
                m = P.pe(lambda e, k=k, i=i, p=p: e.matmul(p.t[:, k, :], zi[i].t[:, blk(k)], C["W"][:, 11, :], start=True,
                                                           stop=True), lz, p.free, sig=(k == NK - 1))
            zi[i].free = [m]
            Y = yi[i].t
            a = P.dve(lambda e, Y=Y, p=p: e.tensor_tensor(Y[:], p.t[:], Y[:], ALU.add), m, ly)
            p.free = [a]
            a = P.pool(lambda e, Y=Y: e.tensor_tensor(Y[:], Y[:], tr[:].unsqueeze(1).to_broadcast([128, NK, 128]), ALU.add), a, u)
            for k in range(NK):
                b = P.dve(lambda e, k=k, g=g, Y=Y: e.scalar_tensor_tensor(
                    Y[:, k, :], Y[:, k, :], C["mf"][:, g * NK + k:g * NK + k + 1], C["rows"][:, 9, :], ALU.mult, ALU.add), a)
            for k in range(NK):
                c = P.dve(lambda e, k=k, g=g, Y=Y, i=i: e.scalar_tensor_tensor(
                    xi[i].t[:, k, :], Y[:, k, :], C["mf"][:, g * NK + k:g * NK + k + 1], xi[i].t[:, k, :], ALU.mult, ALU.add), b, lx)
            yi[i].free = [c]
            xi[i].free = [P.dma("act", och[i], A["out"][g], flat2(xi[i].t), c)]
        P.run()


def kernel(**inputs):
    import concourse.bacc as bacc
    from concourse.bass_utils import run_bass_kernel_spmd as run

    I = {k: np.asarray(v) for k, v in inputs.items()}
    adj = np.ascontiguousarray(I["adj"])
    arrays = {
        "x": np.ascontiguousarray(I["x"].reshape(G, NK, 128, D).transpose(0, 2, 1, 3).reshape(G, 128, N)),
        "adj": adj,
        "adjT": np.ascontiguousarray(adj.transpose(0, 2, 1)),
        "mask": np.ascontiguousarray(I["nodemask"].reshape(G, NK, 128).transpose(2, 0, 1).reshape(128, G * NK)),
    }
    wl = I["L1_gnn_Wl"]
    W = [I["L0_gnn_W0"], I["L0_gnn_W1"], I["L0_gnn_W2"], I["L1_gnn_Wr1"], I["L1_gnn_Wx1"], I["L1_gnn_Wr2"],
         I["L1_gnn_Wx2"], I["L1_gnn_Wr3"], I["L1_gnn_Wx3"], wl[0:128], wl[128:256], wl[256:384]]
    arrays["W"] = np.ascontiguousarray(np.stack(W, 1))
    z = np.zeros(128, np.float32)
    arrays["rows"] = np.ascontiguousarray(np.stack([
        I["L0_gnn_b0"], I["L0_gnn_b1"], I["L0_gnn_b2"], I["L1_gnn_b1"], I["L1_gnn_b2"], I["L1_gnn_b3"], z, z, z,
        I["L1_gnn_bl"], z, z, z]))
    arrays["cols"] = np.ascontiguousarray(np.stack([
        I["L1_gnn_g1"], I["L1_gnn_be1"], I["L1_gnn_g2"], I["L1_gnn_be2"], I["L1_gnn_g3"], I["L1_gnn_be3"]], 1))
    nc = bacc.Bacc("TRN2", target_bir_lowering=False, num_devices=1)
    feed, args = {}, {}
    for name, a in arrays.items():
        feed[f"in_{name}"] = a
        args[name] = nc.dram_tensor(f"in_{name}", a.shape, mybir.dt.from_np(a.dtype), kind="ExternalInput").ap()
    args["out"] = nc.dram_tensor("out_0", (G, 128, N), F32, kind="ExternalOutput").ap()
    build(nc, args)
    r = run(nc, [feed], core_ids=[0])
    o = r.results[0]["out_0"]
    return np.ascontiguousarray(o.reshape(G, 128, NK, D).transpose(0, 2, 1, 3).reshape(G, N, D))
```

```python
from contextlib import ExitStack

import numpy as np
import concourse.bass as bass
from concourse import mybir

F32 = mybir.dt.float32
F32R = mybir.dt.float32r
F16 = mybir.dt.float16
BF16 = mybir.dt.bfloat16
FP8 = mybir.dt.float8e4
U8 = mybir.dt.uint8
I32 = mybir.dt.int32
ALU = mybir.AluOpType
ACT = mybir.ActivationFunctionType
AXX = mybir.AxisListType.X

G = 16
N = 1024
D = 128
NK = 8
MAGIC = 8388608.0
ONE8 = 56.0
ROUNDS = [2, 3, 4, 6, 6, 3, 3, 8]
Q = 4
ENGINES = ("pe", "act", "dve", "pool", "sp")


class Lane:

    def __init__(self, sem):
        self.sem, self.count, self.todo, self.seen = sem, 0, [], {}


class Phase:

    def __init__(self, nc, ctx, name, sems=None):
        self.nc, self.ctx, self.name = nc, ctx, name
        self.sems = {} if sems is None else sems
        self.lanes = {e: Lane(self.sem(e)) for e in ENGINES}
        self.chans = []

    def sem(self, name):
        if name not in self.sems:
            self.sems[name] = self.ctx.enter_context(self.nc.semaphore(f"{self.name}_{name}"))
        return self.sems[name]

    def sb(self, name, shape, dt=F32):
        return self.ctx.enter_context(self.nc.sbuf_tensor(f"{self.name}_{name}", shape, dt))

    def ps(self, name, shape, dt=F32):
        return self.ctx.enter_context(self.nc.psum_tensor(f"{self.name}_{name}", shape, dt))

    def chan(self, name):
        c = [self.sem(name), 0]
        self.chans.append(c)
        return c

    def _put(self, e, fn, waits, sem, by):
        lane = self.lanes[e]
        need = {}
        for s, v in flat(waits):
            if lane.seen.get(s, 0) < v:
                need[s] = max(need.get(s, 0), v)
        lane.seen.update(need)
        lane.todo.append((list(need.items()), fn, sem, by))

    def op(self, e, fn, *waits, sig=True):
        lane = self.lanes[e]
        if sig:
            lane.count += 1
        self._put(e, fn, waits, lane.sem if sig else None, 1)
        return (lane.sem, lane.count) if sig else None

    def pe(self, fn, *waits, sig=True):
        return self.op("pe", fn, *waits, sig=sig)

    def act(self, fn, *waits):
        return self.op("act", fn, *waits)

    def dve(self, fn, *waits):
        return self.op("dve", fn, *waits)

    def pool(self, fn, *waits):
        return self.op("pool", fn, *waits)

    def dma(self, e, chan, out, in_, *waits):
        chan[1] += 16
        self._put(e, lambda q: q.dma_start(out, in_), waits, chan[0], 16)
        return (chan[0], chan[1])

    def run(self):
        for c in self.chans:
            if c[1]:
                self._put("sp", None, [(c[0], c[1])], None, 0)

        def play(e, eng):
            for need, fn, sem, by in self.lanes[e].todo:
                for s, v in need:
                    eng.wait_ge(s, v)
                if fn is not None:
                    ins = fn(eng)
                    if sem is not None:
                        ins.then_inc(sem, by)

        with self.nc.Block() as block:
            block.tensor(lambda eng: play("pe", eng))
            block.scalar(lambda eng: play("act", eng))
            block.vector(lambda eng: play("dve", eng))
            block.gpsimd(lambda eng: play("pool", eng))
            block.sync(lambda eng: play("sp", eng))


def flat(ws):
    for w in ws:
        if w is None:
            continue
        if isinstance(w, tuple) and len(w) == 2 and isinstance(w[1], int):
            yield w
        else:
            yield from flat(w)


class Buf:

    def __init__(self, t):
        self.t, self.free, self.ready = t, [], None


def bc(ap, n):
    return ap.unsqueeze(2).to_broadcast([ap.shape[0], ap.shape[1], n])


def blk(k):
    return slice(k * 128, k * 128 + 128)


def build(nc, A):
    with ExitStack() as top:
        def sb(name, shape, dt=F32):
            return top.enter_context(nc.sbuf_tensor(name, shape, dt))

        C = {}
        C["ident"] = sb("ident", [128, 128])
        C["ident8"] = sb("ident8", [128, 128], FP8)
        C["tri"] = sb("tri", [128, 128], FP8)
        C["U2"] = sb("U2", [128, 132], BF16)
        C["UL"] = sb("UL", [128, N], BF16)
        C["two1"] = sb("two1", [128, 2], BF16)
        C["zero1"] = sb("zero1", [128, 2], BF16)
        C["onesf"] = sb("onesf", [128, 128])
        C["eps"] = sb("eps", [128, 1])
        C["mi"] = sb("mi", [128, 128], I32)
        C["mf"] = sb("mf", [128, 128])
        C["mv"] = sb("mv", [128, 128])
        C["flags"] = sb("flags", [128, 128])
        C["flag"] = sb("flag", [128, 1], I32)
        S = {}
        for n in ("x1", "z1", "z2", "ag1", "ag2", "ya"):
            S[n] = nc.dram_tensor(f"scr_{n}", [G, 128, N], F32, kind="Internal").ap()
        S["keep"] = nc.dram_tensor("scr_keep", [G, NK, 128, N], U8, kind="Internal").ap()

        setup(nc, A, C)
        layer0(nc, A, C, S)
        unsettled = changed(nc, C)
        with nc.If(unsettled > 0):
            dilate_all(nc, A, C, S)
        C["W"] = sb("W", [128, 12, 128])
        C["rows"] = sb("rows", [128, 13, 128])
        C["cols"] = sb("cols", [128, 6])
        C["rdeg"] = sb("rdeg", [128, G, NK])
        C["rho"] = sb("rho", [128, G, NK])
        C["mf2"] = sb("mf2", [128, G * NK])
        weights(nc, A, C)
        layer1_first(nc, A, C, S)
        layer1_next(nc, A, C, S, 2)
        C["z3"] = sb("z3", [128, G, N])
        C["part"] = sb("part", [128, G, N])
        layer1_next(nc, A, C, S, 3)
        final(nc, A, C, S)


def setup(nc, A, C):
    with ExitStack() as ctx:
        P = Phase(nc, ctx, "s")
        ch = P.chan("c")
        m = P.dma("sp", ch, C["mi"][:], A["mask"])
        a = P.dve(lambda e: e.tensor_copy(C["mf"][:], C["mi"][:]), m)
        P.dve(lambda e: e.tensor_scalar(C["mv"][:], C["mf"][:], 0.0, None, ALU.not_equal), a)
        P.dve(lambda e: e.memset(C["eps"][:], 1e-5))
        P.dve(lambda e: e.memset(C["zero1"][:], 0.0))
        P.dve(lambda e: e.memset(C["flags"][:], 0.0))
        P.dve(lambda e: e.memset(C["onesf"][:], 1.0))
        P.dve(lambda e: e.memset(C["two1"][:], 2.0))
        t = P.sb("t", [128, 3, 128])
        i0 = P.pool(lambda e: e.memset(C["ident"][:], 0.0))
        i1 = P.pool(lambda e: e.affine_select(out=C["ident"][:], in_=C["ident"][:], compare_op=ALU.not_equal,
                                              fill=1.0, base=0, pattern=[[-1, 128]], channel_multiplier=1), i0)
        P.dve(lambda e: e.tensor_copy(C["ident8"][:], C["ident"][:], saturate=False), i1)
        z0 = P.pool(lambda e: e.memset(t[:, 0, :], 0.0))
        z1 = P.pool(lambda e: e.affine_select(out=t[:, 0, :], in_=t[:, 0, :], compare_op=ALU.is_ge,
                                              fill=1.0, base=0, pattern=[[-1, 128]], channel_multiplier=1), z0)
        P.dve(lambda e: e.tensor_copy(C["tri"][:], t[:, 0, :], saturate=False), z1)
        z2 = P.pool(lambda e: e.tensor_tensor(t[:, 1, :], t[:, 0, :], C["ident"][:], ALU.add), z1)
        u = P.dve(lambda e: e.memset(C["U2"][:], 1.0))
        P.dve(lambda e: e.tensor_scalar(C["U2"][:, 0:128], t[:, 1, :], 2.0, None, ALU.mult), z2, u)
        u = P.dve(lambda e: e.memset(C["UL"][:], 2.0))
        P.dve(lambda e: e.tensor_scalar(C["UL"][:, 0:128], t[:, 1, :], 2.0, None, ALU.mult), u)
        w = P.dve(lambda e: e.memset(C["two1"][:, 1:2], 1.0))
        P.dve(lambda e: e.memset(C["zero1"][:, 1:2], 1.0), w)
        P.run()


def weights(nc, A, C):
    with ExitStack() as ctx:
        P = Phase(nc, ctx, "w")
        ch = P.chan("c")
        P.dma("sp", ch, C["W"][:], A["W"])
        P.dma("sp", ch, C["rows"][:], A["rows"].partition_broadcast(128))
        P.dma("sp", ch, C["cols"][:], A["cols"])
        P.dve(lambda e: e.tensor_tensor(C["mf2"][:], C["mf"][:], C["mf"][:], ALU.mult))
        P.run()


def col8(t, g):
    return t[:, g * NK:g * NK + NK]


class LayerNorm:

    def __init__(self, P, C):
        self.P, self.C = P, C
        self.st = P.sb("lnst", [128, NK, 6])
        self.mv = P.sb("lnmv", [128, NK, 2])
        self.sd = P.sb("lnsd", [128, NK])
        self.rs = P.sb("lnrs", [128, NK])
        self.last = None

    def __call__(self, x, out, xtok, outfree):
        P = self.P
        a = [P.dve(lambda e, k=k: e.bn_stats(self.st[:, k, :], x[:, k, :]), xtok) for k in range(NK)]
        b = [P.dve(lambda e, k=k: e.bn_aggr(self.mv[:, k, :], self.st[:, k, :]), a[k], self.last) for k in range(NK)]
        s = P.act(lambda e: e.activation(self.sd[:], self.mv[:, :, 1], ACT.Sqrt, bias=self.C["eps"][:, 0:1]), b)
        r = P.dve(lambda e: e.reciprocal(self.rs[:], self.sd[:]), s)
        t = [P.dve(lambda e, k=k: e.tensor_scalar(out[:, k, :], x[:, k, :], self.mv[:, k, 0:1], self.rs[:, k:k + 1],
                                                  ALU.subtract, ALU.mult), r, outfree) for k in range(NK)]
        self.last = t[-1]
        return t[-1]


class RowNorm:

    def __init__(self, P):
        self.P = P
        self.ss = P.sb("rnss", [128, NK])
        self.s2 = P.sb("rns2", [128, NK])
        self.s3 = P.sb("rns3", [128, NK])
        self.rn = P.sb("rnrn", [128, NK])
        self.ssfree, self.last = None, None

    def __call__(self, sq, h, htok, sqfree):
        P = self.P
        a = [P.act(lambda e, k=k: e.activation(sq[:, k, :], h[:, k, :], ACT.Square, accum_out=self.ss[:, k:k + 1]),
                   htok[k], sqfree, self.ssfree) for k in range(NK)]
        c = P.dve(lambda e: e.tensor_scalar(self.s2[:], self.ss[:], 1e-24, None, ALU.max), a)
        self.ssfree = c
        d = P.act(lambda e: e.activation(self.s3[:], self.s2[:], ACT.Sqrt), c)
        return P.dve(lambda e: e.reciprocal(self.rn[:], self.s3[:]), d, self.last), a


def layer0(nc, A, C, S):
    with ExitStack() as ctx:
        P = Phase(nc, ctx, "a")
        W, rows = P.sb("W", [128, 3, 128]), P.sb("rows", [128, 3, 128])
        adj = [Buf(P.sb(f"adj{i}", [128, NK, N])) for i in range(2)]
        adjch = [P.chan(f"adj{i}") for i in range(2)]
        xt, xch, xsch = Buf(P.sb("x", [128, NK, 128])), P.chan("x"), P.chan("xs")
        hT = [Buf(P.sb(f"hT{i}", [128, N])) for i in range(2)]
        Hr = [Buf(P.sb(f"Hr{i}", [128, NK, 128])) for i in range(2)]
        nh = [Buf(P.sb(f"nh{i}", [128, N], F32R)) for i in range(2)]
        nl = [Buf(P.sb(f"nl{i}", [128, N], F32R)) for i in range(2)]
        tmp = Buf(P.sb("tmp", [128, NK, 128]))
        ew = [Buf(P.sb(f"ew{i}", [128, 512])) for i in range(3)]
        acc = [Buf(P.ps(f"acc{i}", [128, 512])) for i in range(2)]
        cos = [Buf(P.ps(f"cos{i}", [128, 512])) for i in range(2)]
        pp = Buf(P.ps("pp", [128, NK, 128]))
        ln = LayerNorm(P, C)
        rn = RowNorm(P)
        dil = Dilation(P, C)
        ch = P.chan("w")
        P.dma("sp", ch, W[:], A["W"][:, 0:3, :])
        wtok = P.dma("sp", ch, rows[:], A["rows"][0:3, :].partition_broadcast(128))

        units = []
        for u in range(3 * G):
            pi, r = divmod(u, 6)
            units.append((2 * pi + r % 2, r // 2))
        adjtok, later = {}, {}

        def load_adj(g):
            b = adj[g % 2]
            adjtok[g] = P.dma("sp", adjch[g % 2], b.t[:], A["adjT"][g].rearrange("(k p) n -> p k n", p=128), b.free)

        def load_x(g):
            xt.ready = P.dma("sp", xch, flat2(xt.t), A["x"][g], xt.free)

        def transposes(src, tok):
            for k in range(NK):
                t = P.pe(lambda e, k=k: e.transpose(pp.t[:, k, :], src(k), C["ident"][:]), tok, pp.free,
                         sig=(k == NK - 1))
            return t

        def prep_ln(g):
            t = ln(xt.t, tmp.t, xt.ready, tmp.free)
            xt.free = [t]

            def rest():
                tt = transposes(lambda k: tmp.t[:, k, :], t)
                tmp.free = [tt]
                h = hT[g % 2]
                ev = P.act(lambda e: e.activation(h.t[:], flat2(pp.t), ACT.Relu), tt, h.free)
                pp.free = [ev]
                h.ready = ev
            return rest

        def prep_h(u):
            g, i = units[u]
            h, H, n, m = hT[g % 2], Hr[g % 2], nh[g % 2], nl[g % 2]
            for k in range(NK):
                t = P.pe(lambda e, k=k: e.matmul(pp.t[:, k, :], h.t[:, blk(k)], W[:, i, :], start=True, stop=True),
                         h.ready, pp.free, wtok, sig=(k == NK - 1))
            h.free = [t]
            H.ready = P.dve(lambda e: e.tensor_tensor(
                H.t[:], pp.t[:], rows[:, i, :].unsqueeze(1).to_broadcast([128, NK, 128]), ALU.add), t, H.free, wtok)
            pp.free = [H.ready]
            r, b = rn(tmp.t, H.t, [H.ready] * NK, tmp.free)
            v = P.dve(lambda e: e.tensor_tensor(tmp.t[:], H.t[:], bc(rn.rn[:], 128), ALU.mult), r, H.ready, b)
            rn.last = v

            def rest():
                tt = transposes(lambda k: tmp.t[:, k, :], v)
                tmp.free = [tt]
                n.ready = P.act(lambda e: e.activation(n.t[:], flat2(pp.t), ACT.Copy), tt, n.free)
                m.ready = P.dve(lambda e: e.tensor_tensor(m.t[:], flat2(pp.t), n.t[:].bitcast(F32), ALU.subtract),
                                n.ready, m.free)
                pp.free = [m.ready]
            return rest

        def evac(u):
            g, i = units[u]
            h = hT[g % 2]
            f = ACT.Relu if i < 2 else ACT.Copy
            for j in range(2):
                t = P.act(lambda e, j=j: e.activation(h.t[:, j * 512:j * 512 + 512], acc[j].t[:], f),
                          acc[j].ready, h.free)
                acc[j].free = [t]
            h.ready = t

        def post(u):
            g, i = units[u]
            h = hT[g % 2]
            tt = transposes(lambda k: h.t[:, blk(k)], h.ready)
            h.free = [tt]
            s = P.dve(lambda e: e.tensor_tensor(xt.t[:], pp.t[:], xt.t[:], ALU.add), tt, xt.ready)
            pp.free = [s]
            xt.free = [P.dma("sp", xsch, S["x1"][g], flat2(xt.t), s)]

        def do_cos(u, k, j):
            g, i = units[u]
            n, m, a, c = nh[g % 2], nl[g % 2], adj[g % 2], cos[j]
            parts = [(n, n), (n, m), (m, n)]
            for x, (l, r) in enumerate(parts):
                t = P.pe(lambda e, l=l, r=r, x=x: e.matmul(c.t[:], l.t[:, blk(k)], r.t[:, j * 512:j * 512 + 512],
                                                           start=(x == 0), stop=(x == 2)),
                         n.ready, m.ready, c.free, sig=(x == 2))
            w = ew[(2 * (u * NK + k) + j) % 3]
            v = P.dve(lambda e: e.tensor_tensor(w.t[:], a.t[:, k, j * 512:j * 512 + 512], c.t[:], ALU.mult),
                      t, w.free, adjtok[g])
            c.free = [v]
            w.ready = v
            if k == NK - 1 and j == 1:
                n.free = m.free = [t]
                if i == 2:
                    a.free = [v]
                    if g + 2 < G:
                        load_adj(g + 2)

        def do_agg(u, k, j):
            g, i = units[u]
            H, w = Hr[g % 2], ew[(2 * (u * NK + k) + j) % 3]
            t = P.pe(lambda e: e.matmul(acc[j].t[:], H.t[:, k, :], w.t[:], start=(k == 0), stop=(k == NK - 1)),
                     w.ready, H.ready, acc[j].free if k == 0 else None)
            w.free = [t]
            acc[j].ready = t
            if k == NK - 1 and j == 1:
                H.free = [t]

        load_x(0)
        load_adj(0)
        load_adj(1)
        prep_ln(0)()
        prep_h(0)()
        first = [(i, k) for k in range(NK) for i in range(Q)]
        for i, k in first[:Q]:
            dil.prep(i, k, A["adjT"][i])
        first = first[Q:]
        stages = [f for q in range(G // Q) for f in dil.stages(q, A, S)]
        lead, total, done = 12, 6 * G * NK, 0

        steps = [(u, k) for u in range(3 * G) for k in range(NK)]
        do_cos(0, 0, 0)
        do_cos(0, 0, 1)
        for s, (u, k) in enumerate(steps):
            ends = u >= 1 and units[u - 1][1] == 2
            g2, i2 = units[u + 1] if u + 1 < 3 * G else (None, None)
            if i2 == 0 and k == 0:
                load_x(g2)
                later["ln"] = prep_ln(g2)
            if ends and k == 0:
                load_x(units[u - 1][0])
            if ends and k == 2:
                post(u - 1)
            if i2 == 0:
                if k == 3:
                    later["ln"]()
                if k == 4:
                    later["h"] = prep_h(u + 1)
                if k == 7:
                    later["h"]()
            elif i2 is not None:
                if k == 1:
                    later["h"] = prep_h(u + 1)
                if k == 5:
                    later["h"]()
            for j in range(2):
                if s + 1 < len(steps):
                    do_cos(*steps[s + 1], j)
                do_agg(u, k, j)
                half = 2 * s + j
                if first and half % 2 == 0:
                    i, kk = first.pop(0)
                    dil.prep(i, kk, A["adjT"][i])
                while done < len(stages) and done * (total - lead) < (half + 1 - lead) * len(stages):
                    stages[done]()
                    done += 1
            if k == NK - 1:
                evac(u)
        load_x(units[-1][0])
        post(3 * G - 1)
        for f in stages[done:]:
            f()
        P.run()


class Dilation:

    def __init__(self, P, C):
        self.C = C
        self.AT = [Buf(P.sb(f"AT{i}", [128, NK, N], FP8)) for i in range(Q)]
        self.R = [Buf(P.sb(f"R{i}", [128, NK, N], FP8)) for i in range(Q)]
        self.ats = [Buf(P.sb(f"ats{i}", [128, 4, 128])) for i in range(2)]
        self.af = [Buf(P.sb(f"af{i}", [128, 512])) for i in range(2)]
        self.Ab = [Buf(P.sb(f"Ab{i}", [128, N], FP8)) for i in range(2 * Q)]
        self.Au = P.sb("Au", [128, 128], FP8)
        self.X = [P.sb(f"X{i}", [128, 128], FP8) for i in range(Q)]
        self.Sd = [[P.sb(f"Sd{i}{j}", [128, 128], FP8) for j in range(2)] for i in range(Q)]
        self.v8 = P.sb("v8", [128, 128], FP8)
        self.base = P.sb("base", [128, 2, 2, 2])
        self.cnt = P.sb("cnt", [128, 2, 2])
        self.vr = P.sb("vr", [128, Q, 128], F16)
        self.v = [Buf(P.sb(f"v{i}", [128, 512], F16)) for i in range(3)]
        self.kp = [Buf(P.sb(f"kp{i}", [128, 512], FP8)) for i in range(2)]
        self.small = {n: P.sb(f"sm_{n}", [128, Q]) for n in ("t", "sf", "sc", "va", "h", "b", "c", "b2")}
        self.D = P.ps("D", [128, 2, 512])
        self.bank = [Buf(self.D[:, b, :]) for b in range(2)]
        self.attach(P)

    def attach(self, P):
        self.P = P
        self.atsch = [P.chan(f"ats{i}") for i in range(2)]
        self.afch = [P.chan(f"af{i}") for i in range(2)]
        self.kpch = [P.chan(f"kp{i}") for i in range(2)]
        for b in (*self.AT, *self.R, *self.ats, *self.af, *self.Ab, *self.v, *self.kp, *self.bank):
            b.free, b.ready = [], None
        self.nv = self.nb = self.nk = 0
        self.smallfree, self.vrfree = [], []
        self.attok = {}
        self.atfree = {}
        self.basetok = self.autok = self.v8tok = self.ruletok = None
        self.xtok, self.xfree = [None] * Q, [None] * Q
        self.sdtok = [[None, None] for _ in range(Q)]
        self.sdfree = [[None, None] for _ in range(Q)]
        self.ranktok = [None] * Q
        self.vrtok = [None] * Q

    def prep(self, i, k, src):
        P, AT = self.P, self.AT[i]
        for h in range(2):
            a = self.ats[h]
            l = P.dma("sp", self.atsch[h], a.t[:], src[h * 512:h * 512 + 512, blk(k)].rearrange("(q p) n -> p q n", p=128),
                      a.free)
            t = P.pool(lambda e, a=a, h=h: e.tensor_scalar(AT.t[:, 4 * h:4 * h + 4, blk(k)].bitcast(U8), a.t[:], 0.0, ONE8,
                                                           ALU.is_gt, ALU.mult), l, self.atfree.get((i, k)))
            a.free = [t]
        self.attok[i, k] = t

    def rowsign(self, i, k, src):
        b = self.Ab[Q * (k % 2) + i]
        for j in range(2):
            a, h = self.af[j], slice(j * 512, j * 512 + 512)
            l = self.P.dma("sp", self.afch[j], a.t[:], src[:, h], a.free)
            b.ready = self.P.act(lambda e, a=a, h=h: e.activation(b.t[:, h], a.t[:], ACT.Sign, saturate=False), l, b.free)
            a.free = [b.ready]

    def rank(self, i):
        return self.D[:, i // 2, (i % 2) * 144:(i % 2) * 144 + 144]

    def count(self, i, src, *waits):
        b = self.bank[i // 2]
        t = self.P.pe(lambda e: e.matmul(self.rank(i)[:, 0:129], src, self.C["U2"][:, 0:129], start=True, stop=True),
                      waits, b.free)
        self.ranktok[i] = t
        return t

    def start(self, i, k):
        P, C = self.P, self.C
        self.k = k
        AT, R, ab = self.AT[i], self.R[i], self.Ab[Q * (k % 2) + i]
        low = at = self.attok.get((i, k))
        if k:
            low = P.dve(lambda e: e.tensor_tensor(AT.t[:, 0:k, blk(k)], AT.t[:, 0:k, blk(k)], R.t[:, 0:k, blk(k)],
                                                  ALU.is_gt, saturate=False), at, R.ready)
        self.attok[i, k] = [at, low]
        au = P.dve(lambda e: e.scalar_tensor_tensor(self.Au[:], ab.t[:, blk(k)], 0.0, C["tri"][:], ALU.max, ALU.mult,
                                                    saturate=False), ab.ready, self.autok)
        self.xtok[i] = self.autok = P.dve(lambda e: e.scalar_tensor_tensor(
            self.X[i][:], AT.t[:, k, blk(k)], 2.0, self.Au[:], ALU.mult, ALU.subtract, saturate=False), at, au, self.xfree[i])
        b = self.bank[i // 2]
        others = [q for q in range(NK) if q != k]
        for q in others:
            t = P.pe(lambda e, q=q: e.matmul(self.rank(i)[:, 132:134], AT.t[:, q, blk(k)],
                                             (C["two1"] if q < k else C["zero1"])[:], start=(q == others[0]),
                                             stop=(q == others[-1])),
                     low, at, b.free, sig=False)
        self.count(i, AT.t[:, k, blk(k)], at)

    def rule(self, mv, first):
        P, C, s = self.P, self.C, self.small
        num, sf, flat4 = self.cnt, s["sf"], self.cnt[:].rearrange("p b i -> p (b i)")
        D = self.D[:, :, 0:288].rearrange("p b (i c) -> p b i c", c=144)
        base = lambda c: self.base[:].rearrange("p b i c -> p (b i) c")[:, :, c]
        if first:
            self.basetok = P.dve(lambda e: e.tensor_copy(self.base[:], D[:, :, :, 132:134]), self.ranktok, self.smallfree)
        n = P.dve(lambda e: e.tensor_tensor(num[:], D[:, :, :, 128], self.base[:, :, :, 1], ALU.add), self.ranktok,
                  self.basetok, self.smallfree)
        a = P.dve(lambda e: e.tensor_scalar(s["t"][:], flat4, 0.5, 0.5, ALU.add, ALU.mult), n)
        c = P.dve(lambda e: e.scalar_tensor_tensor(s["sc"][:], flat4, 10.5, mv, ALU.is_gt, ALU.mult), n)
        d = P.dve(lambda e: e.scalar_tensor_tensor(s["va"][:], flat4, 1.5, mv, ALU.is_gt, ALU.mult), n)
        b = P.dve(lambda e: e.tensor_scalar(sf[:], s["t"][:], MAGIC, MAGIC, ALU.add, ALU.subtract), a)
        q = P.dve(lambda e: e.tensor_tensor(s["c"][:], s["sc"][:], base(0), ALU.mult), c)
        h = P.dve(lambda e: e.scalar_tensor_tensor(s["h"][:], s["sc"][:], -4.0, s["va"][:], ALU.mult, ALU.add), c, d)
        p = P.dve(lambda e: e.tensor_tensor(s["b"][:], sf[:], s["h"][:], ALU.mult), h, b)
        b2 = P.dve(lambda e: e.tensor_tensor(s["b2"][:], s["b"][:], s["c"][:], ALU.add), p, q)
        self.ruletok = [b2, p]
        self.smallfree = []
        self.bank[0].free, self.bank[1].free = [n], [n]
        for i in range(Q):
            t = P.act(lambda e, i=i: e.activation(self.vr[:, i, :], self.rank(i)[:, 0:128], ACT.Abs,
                                                  bias=s["b2"][:, i:i + 1], scale=s["sc"][:, i:i + 1]),
                      self.ranktok, n, self.ruletok, self.vrfree)
            self.vrtok[i] = t
            self.bank[i // 2].free.append(t)
            self.smallfree.append(t)
        self.vrfree = []

    def drop(self, r, last):
        P, s = self.P, self.small
        for i in range(Q):
            new = self.Sd[i][(r + 1) % 2]
            x = P.dve(lambda e, i=i, new=new: e.scalar_tensor_tensor(
                new[:], self.vr[:, i, :], s["sf"][:, i:i + 1], self.X[i][:], ALU.is_equal, ALU.is_lt, saturate=False),
                self.vrtok[i], self.xtok[i], self.sdfree[i][(r + 1) % 2])
            self.sdtok[i][(r + 1) % 2] = x
            self.xfree[i] = x
            self.vrfree.append(x)
            self.smallfree.append(x)
            if not last:
                self.sdfree[i][(r + 1) % 2] = self.count(i, new[:], x)

    def settled(self, i, r, col):
        self.v8tok = self.P.dve(lambda e: e.scalar_tensor_tensor(
            self.v8[:], self.Sd[i][0][:], 1.0, self.Sd[i][1][:], ALU.mult, ALU.not_equal, accum_out=col, saturate=False),
            self.sdtok[i], self.v8tok)

    def wide(self, i, j, r):
        P, C, s, k = self.P, self.C, self.small, self.k
        AT, R, ab = self.AT[i], self.R[i], self.Ab[Q * (k % 2) + i]
        w = self.bank[self.nb % 2]
        v = self.v[self.nv % 3]
        self.nb += 1
        self.nv += 1
        qs = [q for q in range(NK) if q * 128 < j * 512 + 512]
        sd = self.Sd[i][(r + 1) % 2]
        for q in qs:
            lo = max(q * 128, j * 512)
            src = sd[:] if q == k else AT.t[:, q, blk(k)]
            t = P.pe(lambda e, q=q, lo=lo, src=src: e.matmul(
                w.t[:, lo - j * 512:512], src, C["UL"][:, lo - q * 128:j * 512 + 512 - q * 128],
                start=(q == 0), stop=(q == qs[-1]), skip_group_check=True),
                w.free, self.sdtok[i][(r + 1) % 2], self.attok.get((i, k)), sig=(q == qs[-1]))
        a = P.act(lambda e: e.activation(v.t[:], w.t[:], ACT.Abs, bias=s["b"][:, i:i + 1], scale=s["sc"][:, i:i + 1]),
                  t, self.ruletok, v.free)
        w.free = [a]
        self.sdfree[i][(r + 1) % 2] = t
        self.atfree[i, k] = t

        def finish():
            x = P.dve(lambda e: e.scalar_tensor_tensor(
                R.t[:, k, j * 512:j * 512 + 512], v.t[:], s["sf"][:, i:i + 1], ab.t[:, j * 512:j * 512 + 512],
                ALU.not_equal, ALU.is_lt, saturate=False), a, ab.ready, R.free)
            v.free = [x]
            ab.free = [x, self.xtok[i]]
            R.ready = x
            self.smallfree += [a, x]
        return finish

    def mask(self, i, q, j, dst):
        P, C = self.P, self.C
        R, w, kp, ch = self.R[i], self.bank[self.nb % 2], self.kp[self.nk % 2], self.kpch[self.nk % 2]
        self.nb += 1
        self.nk += 1
        P.pe(lambda e: e.matmul(w.t[:], C["ident8"][:], R.t[:, q, j * 512:j * 512 + 512], start=True, stop=False,
                                skip_group_check=True), R.ready, w.free, sig=False)
        for b in range(4):
            t = P.pe(lambda e, b=b: e.matmul(w.t[:, blk(b)], R.t[:, 4 * j + b, blk(q)], C["ident8"][:], start=False,
                                             stop=(b == 3), skip_group_check=True), sig=(b == 3))
        a = P.act(lambda e: e.activation(kp.t[:], w.t[:], ACT.Relu, bias=1.0, scale=-1.0, saturate=False), t, kp.free)
        w.free = [a]
        if q == NK - 1 and j == 1:
            R.free = [t]
        kp.free = [P.dma("sp", ch, dst[:, j * 512:j * 512 + 512], kp.t[:].bitcast(U8), a)]

    def stages(self, quad, A, S):
        C, out, g0 = self.C, [], Q * quad
        mv = C["mv"][:].rearrange("p (g k) -> p g k", k=NK)[:, g0:g0 + Q, :]
        pend = []

        def rows(k):
            for i in range(Q):
                self.rowsign(i, k, A["adj"][g0 + i, blk(k), :])

        def flush():
            while pend:
                pend.pop(0)()

        def wide(i, j, r):
            f = self.wide(i, j, r)
            flush()
            pend.append(f)

        def start(i, k):
            if i == 0 and k == 0:
                rows(0)
            flush()
            self.start(i, k)
            if i == 1 and k + 1 < NK:
                rows(k + 1)

        def check(k, r):
            for i in range(Q):
                c = (g0 + i) * NK + k
                self.settled(i, r, C["flags"][:, c:c + 1])

        def refill(i, k):
            if g0 + Q < G:
                self.prep(i, k, A["adjT"][g0 + Q + i])

        for k in range(NK):
            for i in range(Q):
                out.append(lambda i=i, k=k: start(i, k))
            K = ROUNDS[k]
            for r in range(K):
                out.append(lambda r=r, k=k: self.rule(mv[:, :, k], r == 0))
                out.append(lambda r=r, K=K: self.drop(r, r == K - 1))
            out.append(lambda k=k, K=K: check(k, K - 1))
            for i in range(Q):
                out.append(lambda i=i, k=k, K=K: (wide(i, 0, K - 1), wide(i, 1, K - 1), refill(i, k)))
        out.append(flush)
        for i in range(Q):
            for q in range(NK):
                out.append(lambda i=i, q=q: [self.mask(i, q, j, S["keep"][g0 + i, q]) for j in range(2)])
        return out


def changed(nc, C):
    with ExitStack() as ctx:
        P = Phase(nc, ctx, "n")
        r, ps = P.sb("r", [128, 1]), P.ps("ps", [128, 1])
        a = P.dve(lambda e: e.tensor_reduce(r[:], C["flags"][:], AXX, ALU.add))
        b = P.pe(lambda e: e.matmul(ps[:], C["onesf"][:], r[:], start=True, stop=True), a)
        P.dve(lambda e: e.tensor_copy(C["flag"][:], ps[:]), b)
        P.run()
    return nc.values_load(C["flag"][0:1, 0:1], min_val=0, max_val=128 * 128 * 128)


def dilate_all(nc, A, C, S):
    with ExitStack() as ctx:
        M = Phase(nc, ctx, "g")
        mi, mf, mv = M.sb("mi", [128, Q, NK], I32), M.sb("mf", [128, Q, NK]), M.sb("mv", [128, Q, NK])
        dil = Dilation(M, C)
        M.chan("m")

        def stage(fill):
            P = Phase(nc, ctx, "g", M.sems)
            dil.attach(P)
            fill(P)
            P.run()
            for s in P.sems.values():
                nc.sync.sem_clear(s)
            nc.all_engine_barrier()

        with nc.Fori(0, G // Q) as quad:
            def graph(t, i):
                return t[bass.ds(quad * Q + i, 1)]

            def load(P):
                t = P.dma("sp", P.chan("m"), mi[:].rearrange("p i k -> p (i k)"), A["mask"][:, bass.ds(quad * Q * NK, Q * NK)])
                a = P.dve(lambda e: e.tensor_copy(mf[:], mi[:]), t)
                P.dve(lambda e: e.tensor_scalar(mv[:], mf[:], 0.0, None, ALU.not_equal), a)
                for k in range(NK):
                    for i in range(Q):
                        dil.prep(i, k, graph(A["adjT"], i).rearrange("o n m -> (o n) m"))

            def start(k):
                def fill(P):
                    for i in range(Q):
                        dil.rowsign(i, k, graph(A["adj"], i).rearrange("o n m -> (o n) m")[blk(k), :])
                    for i in range(Q):
                        dil.start(i, k)
                    dil.rule(mv[:, :, k], True)
                    dil.drop(0, False)
                return fill

            def again(k):
                def fill(P):
                    dil.rule(mv[:, :, k], False)
                    dil.drop(0, False)
                return fill

            def wide(P):
                for i in range(Q):
                    for j in range(2):
                        dil.wide(i, j, 0)()

            def masks(i, q):
                def fill(P):
                    for j in range(2):
                        dil.mask(i, q, j, graph(S["keep"], i)[:, q].rearrange("o p n -> (o p) n"))
                return fill

            stage(load)
            for k in range(NK):
                stage(start(k))
                with nc.Fori(0, 127):
                    stage(again(k))
                stage(wide)
            for i in range(Q):
                for q in range(NK):
                    stage(masks(i, q))


class Sage:

    def __init__(self, P, A, C, S, adjs, on_dve=NK):
        self.on_dve = on_dve
        self.P, self.A, self.C, self.S = P, A, C, S
        self.adj = [Buf(P.sb(f"adj{i}", [128, NK, N])) for i in range(adjs)]
        self.adjch = [P.chan(f"adj{i}") for i in range(adjs)]
        self.kp = [Buf(P.sb(f"kp{i}", [128, NK, N], FP8)) for i in range(2)]
        self.kpch = [P.chan(f"kp{i}") for i in range(2)]
        self.acc = [Buf(P.ps(f"acc{i}", [128, 512])) for i in range(2)]
        self.masked = {}
        self.ltok = {}

    def load(self, g):
        P, n = self.P, len(self.adj)
        b, c = self.adj[g % n], self.kp[g % 2]
        a = P.dma("sp", self.adjch[g % n], b.t[:], self.A["adjT"][g].rearrange("(k p) n -> p k n", p=128), b.free)
        m = P.dma("sp", self.kpch[g % 2], c.t[:].bitcast(U8), self.S["keep"][g].rearrange("k p n -> p k n"), c.free)
        self.ltok[g] = [a, m]

    def mask(self, g):
        P, n = self.P, len(self.adj)
        b, c = self.adj[g % n], self.kp[g % 2]
        self.masked[g] = [(P.dve if q < self.on_dve else P.pool)(
            lambda e, q=q: e.tensor_tensor(b.t[:, q, :], b.t[:, q, :], c.t[:, q, :], ALU.mult), self.ltok[g])
            for q in range(NK)]
        c.free = self.masked[g]

    def agg(self, g, rows, tok):
        P, b = self.P, self.adj[g % len(self.adj)]
        for q in range(NK):
            for j in range(2):
                t = P.pe(lambda e, q=q, j=j: e.matmul(self.acc[j].t[:], rows[:, q, :], b.t[:, q, j * 512:j * 512 + 512],
                                                      start=(q == 0), stop=(q == NK - 1)),
                         tok, self.masked[g][q], self.acc[j].free if q == 0 else None, sig=(q == NK - 1))
                self.acc[j].ready = t
        return t

    def evac(self, dst, free):
        P = self.P
        for j in range(2):
            t = P.act(lambda e, j=j: e.activation(dst[:, j * 512:j * 512 + 512], self.acc[j].t[:], ACT.Copy),
                      self.acc[j].ready, free)
            self.acc[j].free = [t]
        return t


def flat2(t):
    return t[:].rearrange("p k d -> p (k d)")


class Dense:

    def __init__(self, P, C, transposed):
        self.P, self.C = P, C
        self.p1 = Buf(P.ps("p1", [128, NK, 128]))
        self.p2 = Buf(P.ps("p2", [128, NK, 128]))
        self.o = Buf(P.sb("o", [128, NK, 128]))
        self.sq = P.sb("sq", [128, NK, 128])
        self.z = [Buf(P.sb(f"z{i}", [128, NK, 128])) for i in range(2)]
        self.zT = transposed
        self.rn = RowNorm(P)
        self.rm = P.sb("rm", [128, NK])
        self.sqfree = None

    def mm(self, dst, lhsT, rhs, *waits):
        P = self.P
        for k in range(NK):
            t = P.pe(lambda e, k=k: e.matmul(dst.t[:, k, :], lhsT[:, blk(k)], rhs, start=True, stop=True),
                     waits, dst.free, sig=(k == NK - 1))
        return t

    def products(self, aggT, hT, Wr, Wx, waits):
        self.a = self.mm(self.p1, aggT, Wr, waits)
        self.b = self.mm(self.p2, hT, Wx, waits)
        return self.a, self.b

    def rows(self, g, bias, rank1=None):
        P, C, o, z = self.P, self.C, self.o, self.z[g % 2]
        c = P.dve(lambda e: e.tensor_tensor(o.t[:], self.p2.t[:], bias.unsqueeze(1).to_broadcast([128, NK, 128]),
                                            ALU.add), self.b, o.free)
        self.p2.free = [c]
        f = [P.dve(lambda e, k=k: e.scalar_tensor_tensor(o.t[:, k, :], self.p1.t[:, k, :], C["rdeg"][:, g, k:k + 1],
                                                         o.t[:, k, :], ALU.mult, ALU.add), self.a, c) for k in range(NK)]
        self.p1.free = [f[-1]]
        if rank1 is not None:
            f = [P.dve(lambda e, k=k: e.scalar_tensor_tensor(o.t[:, k, :], rank1, C["rho"][:, g, k:k + 1],
                                                             o.t[:, k, :], ALU.mult, ALU.add), f[k]) for k in range(NK)]
        r, s = self.rn(self.sq, o.t, f, self.sqfree)
        self.sqfree = s[-1]
        m = P.dve(lambda e: e.tensor_tensor(self.rm[:], self.rn.rn[:], col8(C["mf"], g), ALU.mult), r, o.free)
        self.rn.last = m
        z.ready = [P.act(lambda e, k=k: e.activation(z.t[:, k, :], o.t[:, k, :], ACT.Relu, scale=self.rm[:, k:k + 1]),
                         m, f[k], z.free) for k in range(NK)]
        o.free = [z.ready[-1]]
        z.free = []

    def turn(self, g, stats):
        P, z, zT = self.P, self.z[g % 2], self.zT(g)
        for k in range(NK):
            t = P.pe(lambda e, k=k: e.transpose(self.p2.t[:, k, :], z.t[:, k, :], self.C["ident"][:]), z.ready,
                     self.p2.free, sig=(k == NK - 1))
        z.free.append(t)
        zT.ready = P.act(lambda e: e.activation(zT.t[:], flat2(self.p2.t), ACT.Copy), t, zT.free)
        self.p2.free = [zT.ready]
        zT.free = [P.dve(lambda e, j=j: e.bn_stats(stats[:, 2 * g + j, :], zT.t[:, j * 512:j * 512 + 512]), zT.ready)
                   for j in range(2)]


def pair(bufs):
    return lambda g: bufs[g % 2]


def layer1_first(nc, A, C, S):
    with ExitStack() as ctx:
        P = Phase(nc, ctx, "b")
        sg = Sage(P, A, C, S, 3)
        dn = Dense(P, C, pair([Buf(P.sb(f"zT{i}", [128, N])) for i in range(2)]))
        ln = LayerNorm(P, C)
        stats = nc_stats(P, C)
        x = [Buf(P.sb(f"x{i}", [128, NK, 128])) for i in range(2)]
        xch = [P.chan(f"x{i}") for i in range(2)]
        h = [Buf(P.sb(f"h{i}", [128, NK, 128])) for i in range(2)]
        hT, aT = Buf(P.sb("hT", [128, N])), Buf(P.sb("aT", [128, N]))
        a1 = Buf(P.sb("a1", [128, N]))
        a1ch = P.chan("a1")
        zch = [P.chan(f"z{i}") for i in range(2)]
        dsums = [Buf(P.sb(f"dsum{i}", [128, N])) for i in range(2)]
        dg = P.sb("dg", [128, NK])
        dp = P.ps("dp", [128, NK])
        pt = dn.p1
        xtok, degfree = {}, []

        def load(g):
            xtok[g] = P.dma("sp", xch[g % 2], flat2(x[g % 2].t), S["x1"][g], x[g % 2].free)
            sg.load(g)

        def prep(g):
            hb = h[g % 2]
            t = ln(x[g % 2].t, x[g % 2].t, xtok[g], None)
            hb.ready = P.act(lambda e: e.activation(hb.t[:], x[g % 2].t[:], ACT.Relu), t, hb.free)
            x[g % 2].free = [hb.ready]
            hb.free = []
            sg.mask(g)
            b = sg.adj[g % 3]
            m, dsum = sg.masked[g], dsums[g % 2]
            d = P.pool(lambda e: e.tensor_tensor(dsum.t[:], b.t[:, 0, :], b.t[:, 1, :], ALU.add), m[0], m[1], dsum.free)
            for q in range(2, NK):
                d = P.pool(lambda e, q=q: e.tensor_tensor(dsum.t[:], dsum.t[:], b.t[:, q, :], ALU.add), d, m[q])
            b.pool = d
            dsum.ready = d

        def degree(g):
            dsum = dsums[g % 2]
            for k in range(NK):
                t = P.pe(lambda e, k=k: e.matmul(dp[:, k:k + 1], dsum.t[:, blk(k)], C["onesf"][:, 0:1], start=True,
                                                 stop=True), dsum.ready, degfree, sig=(k == NK - 1))
            dsum.free = [t]
            a = P.dve(lambda e: e.tensor_scalar(dg[:], dp[:], 1.0, None, ALU.max), t, degfree)
            b = P.dve(lambda e: e.reciprocal(C["rdeg"][:, g, :], dg[:]), a)
            c = P.dve(lambda e: e.tensor_tensor(C["rho"][:, g, :], dp[:], C["rdeg"][:, g, :], ALU.mult), b)
            degfree[:] = [b, c]

        load(0)
        load(1)
        prep(0)
        load(2)
        for g in range(G + 1):
            if g < G:
                hb = h[g % 2]
                t = sg.agg(g, hb.t, hb.ready)
                hb.free.append(t)
                for k in range(NK):
                    t = P.pe(lambda e, k=k, hb=hb: e.transpose(pt.t[:, k, :], hb.t[:, k, :], C["ident"][:]), hb.ready,
                             pt.free, sig=(k == NK - 1))
                hb.free.append(t)
                aT.ready = sg.evac(aT.t, aT.free)
                hT.ready = P.act(lambda e: e.activation(hT.t[:], flat2(pt.t), ACT.Copy), t, hT.free)
                pt.free = [hT.ready]
            if g + 1 < G:
                prep(g + 1)
            if g:
                dn.turn(g - 1, stats)
                z, zT, b = dn.z[(g - 1) % 2], dn.zT(g - 1), sg.adj[(g - 1) % 3]
                zT.free.append(P.dma("act", zch[(g - 1) % 2], S["z1"][g - 1], zT.t[:], zT.ready))
                t = sg.agg(g - 1, z.t, z.ready)
                z.free.append(t)
                b.free = [t, b.pool]
                e = sg.evac(a1.t, a1.free)
                a1.free = [P.dma("act", a1ch, S["ag1"][g - 1], a1.t[:], e)]
                if g + 2 < G:
                    load(g + 2)
            if g < G:
                degree(g)
                a, b = dn.products(aT.t, hT.t, C["W"][:, 3, :], C["W"][:, 4, :], [aT.ready, hT.ready])
                aT.free, hT.free = [a], [b]
                dn.rows(g, C["rows"][:, 3, :])
        fold(P, C, stats, 1, st_all(P, dn))
        P.run()


def nc_stats(P, C):
    return P.sb("stats", [128, 2 * G, 6])


def st_all(P, dn):
    return [(P.lanes["dve"].sem, P.lanes["dve"].count)]


def fold(P, C, stats, l, waits):
    ag = P.sb("ag", [128, 2])
    sd = P.sb("bsd", [128, 1])
    rs = P.sb("brs", [128, 1])
    s = P.sb("bs", [128, 1])
    ms = P.sb("bms", [128, 1])
    t = P.sb("bt", [128, 1])
    tb = P.sb("btb", [128, 128])
    pv = P.ps("pv", [128, 128])
    a = P.dve(lambda e: e.bn_aggr(ag[:], stats[:].rearrange("p a b -> p (a b)")), waits)
    b = P.act(lambda e: e.activation(sd[:], ag[:, 1:2], ACT.Sqrt, bias=C["eps"][:, 0:1]), a)
    c = P.dve(lambda e: e.reciprocal(rs[:], sd[:]), b)
    d = P.dve(lambda e: e.tensor_tensor(s[:], rs[:], C["cols"][:, 2 * (l - 1):2 * l - 1], ALU.mult), c)
    f = P.dve(lambda e: e.tensor_tensor(ms[:], ag[:, 0:1], s[:], ALU.mult), d)
    h = P.dve(lambda e: e.tensor_tensor(t[:], C["cols"][:, 2 * l - 1:2 * l], ms[:], ALU.subtract), f)
    k = P.dve(lambda e: e.tensor_scalar(tb[:], C["onesf"][:], t[:, 0:1], None, ALU.mult), h)
    use = [(8 + l, 9 + l)] if l == 3 else [(3 + 2 * l, 6), (4 + 2 * l, 3 + l), (8 + l, 9 + l)]
    free = None
    for w, row in use:
        m = P.pe(lambda e, w=w: e.matmul(pv[:], tb[:], C["W"][:, w, :], start=True, stop=True), k, free)
        if row == 6:
            free = P.dve(lambda e: e.tensor_copy(C["rows"][:, 6, :], pv[:]), m)
        else:
            free = P.dve(lambda e, row=row: e.tensor_tensor(C["rows"][:, row, :], C["rows"][:, row, :], pv[:], ALU.add), m)
        P.dve(lambda e, w=w: e.tensor_scalar(C["W"][:, w, :], C["W"][:, w, :], s[:, 0:1], None, ALU.mult), m, d)


def layer1_next(nc, A, C, S, l):
    with ExitStack() as ctx:
        P = Phase(nc, ctx, f"c{l}")
        sums, nb = l == 2, 3 if l == 2 else 2
        sg = Sage(P, A, C, S, 3, 4) if sums else None
        stats = nc_stats(P, C)
        if sums:
            dn = Dense(P, C, pair([Buf(P.sb(f"zT{i}", [128, N])) for i in range(2)]))
            y, yb = Buf(P.sb("y", [128, NK, 128])), Buf(P.sb("yb", [128, NK, 128]))
            py = dn.p1
        else:
            z3 = [Buf(C["z3"][:, g, :]) for g in range(G)]
            dn = Dense(P, C, lambda g: z3[g])
            py = Buf(P.ps("py", [128, NK, 128]))
            yi, yich = [Buf(P.sb(f"yi{i}", [128, NK, 128])) for i in range(2)], [P.chan(f"yi{i}") for i in range(2)]
            xi, xich = [Buf(P.sb(f"xi{i}", [128, NK, 128])) for i in range(2)], [P.chan(f"xi{i}") for i in range(2)]
        zi = [Buf(P.sb(f"zi{i}", [128, N])) for i in range(nb)]
        zich = [P.chan(f"zi{i}") for i in range(nb)]
        ai = [Buf(P.sb(f"ai{i}", [128, N])) for i in range(nb)]
        aich = [P.chan(f"ai{i}") for i in range(nb)]
        zch = [P.chan(f"z{i}") for i in range(2)]
        ych = P.chan("y")
        a2 = Buf(P.sb("a2", [128, N])) if sums else None
        a2ch = P.chan("a2")
        tok = {}

        def load(g):
            i = g % nb
            tok[g] = [P.dma("sp", zich[i], zi[i].t[:], S[f"z{l - 1}"][g], zi[i].free),
                      P.dma("sp", aich[i], ai[i].t[:], S[f"ag{l - 1}"][g], ai[i].free)]
            if sums:
                sg.load(g)
            else:
                yi[i].ready = P.dma("sp", yich[i], flat2(yi[i].t), S["ya"][g], yi[i].free)
                xi[i].ready = P.dma("sp", xich[i], flat2(xi[i].t), S["x1"][g], xi[i].free)

        def layer(g):
            i = g % nb
            a, b = dn.products(ai[i].t, zi[i].t, C["W"][:, 1 + 2 * l, :], C["W"][:, 2 + 2 * l, :], tok[g])
            ai[i].free, zi[i].free = [a], [b]
            dn.rows(g, C["rows"][:, 2 + l, :], C["rows"][:, 6, :])

        def out_product(g):
            i = g % nb
            m = dn.mm(py, zi[i].t, C["W"][:, 7 + l, :], tok[g])
            zi[i].free.append(m)
            return m

        def out_store(g, m):
            e = [P.act(lambda e, k=k: e.activation(y.t[:, k, :], py.t[:, k, :], ACT.Copy,
                                                   scale=C["mf2"][:, g * NK + k:g * NK + k + 1]), m, y.free)
                 for k in range(NK)]
            py.free = [e[-1]]
            b = P.pool(lambda e: e.tensor_tensor(yb.t[:], C["rows"][:, 9, :].unsqueeze(1).to_broadcast([128, NK, 128]),
                                                 bc(col8(C["mf"], g), 128), ALU.mult), yb.free)
            b = P.pool(lambda e: e.tensor_tensor(yb.t[:], yb.t[:], y.t[:], ALU.add), b, e)
            y.free = [b]
            yb.free = [P.dma("act", ych, S["ya"][g], flat2(yb.t), b)]

        def out_part(g, m):
            Y, X = yi[g % 2], xi[g % 2]
            e = P.pool(lambda e: e.tensor_tensor(Y.t[:], Y.t[:], X.t[:], ALU.add), Y.ready, X.ready)
            for k in range(NK):
                t = P.dve(lambda e, k=k: e.scalar_tensor_tensor(
                    C["part"][:, g, blk(k)], py.t[:, k, :], C["mf2"][:, g * NK + k:g * NK + k + 1], Y.t[:, k, :],
                    ALU.mult, ALU.add), e, m)
            py.free = [t]
            Y.free, X.free = [t], [e]

        def turn(g):
            dn.turn(g, stats)
            if sums:
                zT = dn.zT(g)
                zT.free.append(P.dma("act", zch[g % 2], S["z2"][g], zT.t[:], zT.ready))

        load(0)
        load(1)
        if sums:
            for g in range(G + 1):
                if g:
                    turn(g - 1)
                if g < G:
                    layer(g)
                if g:
                    z = dn.z[(g - 1) % 2]
                    t = sg.agg(g - 1, z.t, z.ready)
                    z.free.append(t)
                    sg.adj[(g - 1) % 3].free = [t]
                    e = sg.evac(a2.t, a2.free)
                    a2.free = [P.dma("act", a2ch, S["ag2"][g - 1], a2.t[:], e)]
                if g < G:
                    sg.mask(g)
                    out_store(g, out_product(g))
                if g + 2 < G:
                    load(g + 2)
        else:
            for g in range(G + 1):
                if g < G:
                    layer(g)
                    out_part(g, out_product(g))
                if g:
                    turn(g - 1)
                if g + 2 < G:
                    load(g + 2)
        fold(P, C, stats, l, st_all(P, dn))
        P.run()


def final(nc, A, C, S):
    with ExitStack() as ctx:
        P = Phase(nc, ctx, "f")
        tr = P.sb("tr", [128, 128])
        u = P.dve(lambda e: e.tensor_tensor(tr[:], C["rows"][:, 10, :], C["rows"][:, 11, :], ALU.add))
        u = P.dve(lambda e: e.tensor_tensor(tr[:], tr[:], C["rows"][:, 12, :], ALU.add), u)
        och = P.chan("o")
        pp = [Buf(P.ps(f"p{i}", [128, NK, 128])) for i in range(4)]
        for g in range(G):
            p = pp[g % 4]
            for k in range(NK):
                P.pe(lambda e, k=k, g=g, p=p: e.matmul(p.t[:, k, :], C["z3"][:, g, blk(k)], C["W"][:, 11, :], start=True,
                                                       stop=False, skip_group_check=True), p.free, sig=False)
                m = P.pe(lambda e, k=k, p=p: e.matmul(p.t[:, k, :], C["onesf"][0:1, :], tr[0:1, :], start=False, stop=True,
                                                      skip_group_check=True), u, sig=(k == NK - 1))
            for k in range(NK):
                c = P.dve(lambda e, k=k, g=g, p=p: e.scalar_tensor_tensor(
                    C["part"][:, g, blk(k)], p.t[:, k, :], C["mf2"][:, g * NK + k:g * NK + k + 1],
                    C["part"][:, g, blk(k)], ALU.mult, ALU.add), m)
            p.free = [c]
            P.dma("sp", och, A["out"][g], C["part"][:, g, :], c)
        P.run()


def kernel(**inputs):
    import concourse.bacc as bacc
    from concourse.bass_utils import run_bass_kernel_spmd as run

    I = {k: np.asarray(v) for k, v in inputs.items()}
    adj = np.ascontiguousarray(I["adj"])
    arrays = {
        "x": np.ascontiguousarray(I["x"].reshape(G, NK, 128, D).transpose(0, 2, 1, 3).reshape(G, 128, N)),
        "adj": adj,
        "adjT": np.ascontiguousarray(adj.transpose(0, 2, 1)),
        "mask": np.ascontiguousarray(I["nodemask"].reshape(G, NK, 128).transpose(2, 0, 1).reshape(128, G * NK)),
    }
    wl = I["L1_gnn_Wl"]
    W = [I["L0_gnn_W0"], I["L0_gnn_W1"], I["L0_gnn_W2"], I["L1_gnn_Wr1"], I["L1_gnn_Wx1"], I["L1_gnn_Wr2"],
         I["L1_gnn_Wx2"], I["L1_gnn_Wr3"], I["L1_gnn_Wx3"], wl[0:128], wl[128:256], wl[256:384]]
    arrays["W"] = np.ascontiguousarray(np.stack(W, 1))
    z = np.zeros(128, np.float32)
    arrays["rows"] = np.ascontiguousarray(np.stack([
        I["L0_gnn_b0"], I["L0_gnn_b1"], I["L0_gnn_b2"], I["L1_gnn_b1"], I["L1_gnn_b2"], I["L1_gnn_b3"], z, z, z,
        I["L1_gnn_bl"], z, z, z]))
    arrays["cols"] = np.ascontiguousarray(np.stack([
        I["L1_gnn_g1"], I["L1_gnn_be1"], I["L1_gnn_g2"], I["L1_gnn_be2"], I["L1_gnn_g3"], I["L1_gnn_be3"]], 1))
    nc = bacc.Bacc("TRN2", target_bir_lowering=False, num_devices=1)
    feed, args = {}, {}
    for name, a in arrays.items():
        feed[f"in_{name}"] = a
        args[name] = nc.dram_tensor(f"in_{name}", a.shape, mybir.dt.from_np(a.dtype), kind="ExternalInput").ap()
    args["out"] = nc.dram_tensor("out_0", (G, 128, N), F32, kind="ExternalOutput").ap()
    build(nc, args)
    r = run(nc, [feed], core_ids=[0])
    o = r.results[0]["out_0"]
    return np.ascontiguousarray(o.reshape(G, 128, NK, D).transpose(0, 2, 1, 3).reshape(G, N, D))
```

```python
from contextlib import ExitStack

import numpy as np
import concourse.bass as bass
from concourse import mybir

F32 = mybir.dt.float32
F32R = mybir.dt.float32r
F16 = mybir.dt.float16
BF16 = mybir.dt.bfloat16
FP8 = mybir.dt.float8e4
U8 = mybir.dt.uint8
I32 = mybir.dt.int32
ALU = mybir.AluOpType
ACT = mybir.ActivationFunctionType
AXX = mybir.AxisListType.X

G = 16
N = 1024
D = 128
NK = 8
MAGIC = 8388608.0
ONE8 = 56.0
ROUNDS = [2, 3, 4, 6, 6, 3, 3, 8]
Q = 4
ENGINES = ("pe", "act", "dve", "pool", "sp")


class Lane:

    def __init__(self, sem):
        self.sem, self.count, self.todo, self.seen = sem, 0, [], {}


class Phase:

    def __init__(self, nc, ctx, name, sems=None):
        self.nc, self.ctx, self.name = nc, ctx, name
        self.sems = {} if sems is None else sems
        self.lanes = {e: Lane(self.sem(e)) for e in ENGINES}
        self.chans = []

    def sem(self, name):
        if name not in self.sems:
            self.sems[name] = self.ctx.enter_context(self.nc.semaphore(f"{self.name}_{name}"))
        return self.sems[name]

    def sb(self, name, shape, dt=F32):
        return self.ctx.enter_context(self.nc.sbuf_tensor(f"{self.name}_{name}", shape, dt))

    def ps(self, name, shape, dt=F32):
        return self.ctx.enter_context(self.nc.psum_tensor(f"{self.name}_{name}", shape, dt))

    def chan(self, name):
        c = [self.sem(name), 0]
        self.chans.append(c)
        return c

    def _put(self, e, fn, waits, sem, by):
        lane = self.lanes[e]
        need = {}
        for s, v in flat(waits):
            if lane.seen.get(s, 0) < v:
                need[s] = max(need.get(s, 0), v)
        lane.seen.update(need)
        lane.todo.append((list(need.items()), fn, sem, by))

    def op(self, e, fn, *waits, sig=True):
        lane = self.lanes[e]
        if sig:
            lane.count += 1
        self._put(e, fn, waits, lane.sem if sig else None, 1)
        return (lane.sem, lane.count) if sig else None

    def pe(self, fn, *waits, sig=True):
        return self.op("pe", fn, *waits, sig=sig)

    def act(self, fn, *waits):
        return self.op("act", fn, *waits)

    def dve(self, fn, *waits):
        return self.op("dve", fn, *waits)

    def pool(self, fn, *waits):
        return self.op("pool", fn, *waits)

    def dma(self, e, chan, out, in_, *waits):
        chan[1] += 16
        self._put(e, lambda q: q.dma_start(out, in_), waits, chan[0], 16)
        return (chan[0], chan[1])

    def run(self):
        for c in self.chans:
            if c[1]:
                self._put("sp", None, [(c[0], c[1])], None, 0)

        def play(e, eng):
            for need, fn, sem, by in self.lanes[e].todo:
                for s, v in need:
                    eng.wait_ge(s, v)
                if fn is not None:
                    ins = fn(eng)
                    if sem is not None:
                        ins.then_inc(sem, by)

        with self.nc.Block() as block:
            block.tensor(lambda eng: play("pe", eng))
            block.scalar(lambda eng: play("act", eng))
            block.vector(lambda eng: play("dve", eng))
            block.gpsimd(lambda eng: play("pool", eng))
            block.sync(lambda eng: play("sp", eng))


def flat(ws):
    for w in ws:
        if w is None:
            continue
        if isinstance(w, tuple) and len(w) == 2 and isinstance(w[1], int):
            yield w
        else:
            yield from flat(w)


class Buf:

    def __init__(self, t):
        self.t, self.free, self.ready = t, [], None


def bc(ap, n):
    return ap.unsqueeze(2).to_broadcast([ap.shape[0], ap.shape[1], n])


def blk(k):
    return slice(k * 128, k * 128 + 128)


def build(nc, A):
    with ExitStack() as top:
        def sb(name, shape, dt=F32):
            return top.enter_context(nc.sbuf_tensor(name, shape, dt))

        C = {}
        C["ident"] = sb("ident", [128, 128])
        C["ident8"] = sb("ident8", [128, 128], FP8)
        C["tri"] = sb("tri", [128, 128], FP8)
        C["U2"] = sb("U2", [128, 132], BF16)
        C["UL"] = sb("UL", [128, 512], BF16)
        C["two1"] = sb("two1", [128, 2], BF16)
        C["zero1"] = sb("zero1", [128, 2], BF16)
        C["eps"] = sb("eps", [128, 1])
        C["mf"] = sb("mf", [128, 128])
        C["mv"] = sb("mv", [128, 128])
        C["flags"] = sb("flags", [128, 128])
        C["flag"] = sb("flag", [128, 1], I32)
        S = {}
        for n in ("x1", "z1", "z2", "ag1", "ag2"):
            S[n] = nc.dram_tensor(f"scr_{n}", [G, 128, N], F32, kind="Internal").ap()
        S["keep"] = nc.dram_tensor("scr_keep", [G, NK, 128, N], U8, kind="Internal").ap()

        C["adj"] = [sb(f"adj{i}", [128, NK, N]) for i in range(2)]
        setup(nc, A, C)
        layer0(nc, A, C, S)
        unsettled = changed(nc, C)
        with nc.If(unsettled > 0):
            dilate_all(nc, A, C, S)
        C["adj"].append(sb("adj2", [128, NK, N]))
        C["onesf"] = sb("onesf", [128, 128])
        C["W"] = sb("W", [128, 12, 128])
        C["rows"] = sb("rows", [128, 10, 128])
        C["cols"] = sb("cols", [128, 6])
        C["rdeg"] = sb("rdeg", [128, G, NK])
        C["rho"] = sb("rho", [128, G, NK])
        C["mf2"] = sb("mf2", [128, G * NK])
        C["s"], C["t"] = sb("bn_s", [128, 3]), sb("bn_t", [128, 3])
        weights(nc, A, C)
        layer1_first(nc, A, C, S)
        layer1_next(nc, A, C, S, 2)
        C["adj"].append(sb("adj3", [128, NK, N]))
        C["z3"] = [C["adj"][g // NK][:, g % NK, :] for g in range(G)]
        C["part"] = [C["adj"][2 + g // NK][:, g % NK, :] for g in range(G)]
        layer1_next(nc, A, C, S, 3)
        final(nc, A, C, S)


def setup(nc, A, C):
    with ExitStack() as ctx:
        P = Phase(nc, ctx, "s")
        mi = P.sb("mi", [128, 128], I32)
        ch = P.chan("c")
        m = P.dma("sp", ch, mi[:], A["mask"])
        a = P.dve(lambda e: e.tensor_copy(C["mf"][:], mi[:]), m)
        P.dve(lambda e: e.tensor_scalar(C["mv"][:], C["mf"][:], 0.0, None, ALU.not_equal), a)
        P.dve(lambda e: e.memset(C["eps"][:], 1e-5))
        P.dve(lambda e: e.memset(C["zero1"][:], 0.0))
        P.dve(lambda e: e.memset(C["flags"][:], 0.0))
        P.dve(lambda e: e.memset(C["two1"][:], 2.0))
        t = P.sb("t", [128, 3, 128])
        i0 = P.pool(lambda e: e.memset(C["ident"][:], 0.0))
        i1 = P.pool(lambda e: e.affine_select(out=C["ident"][:], in_=C["ident"][:], compare_op=ALU.not_equal,
                                              fill=1.0, base=0, pattern=[[-1, 128]], channel_multiplier=1), i0)
        P.dve(lambda e: e.tensor_copy(C["ident8"][:], C["ident"][:], saturate=False), i1)
        z0 = P.pool(lambda e: e.memset(t[:, 0, :], 0.0))
        z1 = P.pool(lambda e: e.affine_select(out=t[:, 0, :], in_=t[:, 0, :], compare_op=ALU.is_ge,
                                              fill=1.0, base=0, pattern=[[-1, 128]], channel_multiplier=1), z0)
        P.dve(lambda e: e.tensor_copy(C["tri"][:], t[:, 0, :], saturate=False), z1)
        z2 = P.pool(lambda e: e.tensor_tensor(t[:, 1, :], t[:, 0, :], C["ident"][:], ALU.add), z1)
        u = P.dve(lambda e: e.memset(C["U2"][:], 1.0))
        P.dve(lambda e: e.tensor_scalar(C["U2"][:, 0:128], t[:, 1, :], 2.0, None, ALU.mult), z2, u)
        u = P.dve(lambda e: e.memset(C["UL"][:], 2.0))
        P.dve(lambda e: e.tensor_scalar(C["UL"][:, 0:128], t[:, 1, :], 2.0, None, ALU.mult), u)
        w = P.dve(lambda e: e.memset(C["two1"][:, 1:2], 1.0))
        P.dve(lambda e: e.memset(C["zero1"][:, 1:2], 1.0), w)
        P.run()


def weights(nc, A, C):
    with ExitStack() as ctx:
        P = Phase(nc, ctx, "w")
        ch = P.chan("c")
        P.dma("sp", ch, C["W"][:], A["W"])
        P.dma("sp", ch, C["rows"][:], A["rows"].partition_broadcast(128))
        P.dma("sp", ch, C["cols"][:], A["cols"])
        P.dve(lambda e: e.memset(C["onesf"][:], 1.0))
        P.dve(lambda e: e.tensor_tensor(C["mf2"][:], C["mf"][:], C["mf"][:], ALU.mult))
        P.run()


def col8(t, g):
    return t[:, g * NK:g * NK + NK]


class LayerNorm:

    def __init__(self, P, C):
        self.P, self.C = P, C
        self.st = P.sb("lnst", [128, NK, 6])
        self.mv = P.sb("lnmv", [128, NK, 2])
        self.sd = P.sb("lnsd", [128, NK])
        self.rs = P.sb("lnrs", [128, NK])
        self.last = None

    def __call__(self, x, out, xtok, outfree):
        return self.rows(x, out, self.moments(x, xtok), outfree)

    def moments(self, x, xtok):
        P = self.P
        a = [P.dve(lambda e, k=k: e.bn_stats(self.st[:, k, :], x[:, k, :]), xtok) for k in range(NK)]
        b = [P.dve(lambda e, k=k: e.bn_aggr(self.mv[:, k, :], self.st[:, k, :]), a[k], self.last) for k in range(NK)]
        return P.act(lambda e: e.activation(self.sd[:], self.mv[:, :, 1], ACT.Sqrt, bias=self.C["eps"][:, 0:1]), b)

    def rows(self, x, out, s, outfree):
        P = self.P
        r = P.dve(lambda e: e.reciprocal(self.rs[:], self.sd[:]), s)
        t = [P.dve(lambda e, k=k: e.tensor_scalar(out[:, k, :], x[:, k, :], self.mv[:, k, 0:1], self.rs[:, k:k + 1],
                                                  ALU.subtract, ALU.mult), r, outfree) for k in range(NK)]
        self.last = t[-1]
        return t[-1]


class RowNorm:

    def __init__(self, P):
        self.P = P
        self.ss = P.sb("rnss", [128, NK])
        self.s2 = P.sb("rns2", [128, NK])
        self.s3 = P.sb("rns3", [128, NK])
        self.rn = P.sb("rnrn", [128, NK])
        self.ssfree, self.last = None, None

    def __call__(self, sq, h, htok, sqfree):
        a = self.sums(sq, h, htok, sqfree)
        return self.inverse(self.root(a)), a

    def sums(self, sq, h, htok, sqfree):
        P = self.P
        return [P.act(lambda e, k=k: e.activation(sq[:, k, :], h[:, k, :], ACT.Square, accum_out=self.ss[:, k:k + 1]),
                      htok[k], sqfree, self.ssfree) for k in range(NK)]

    def root(self, a):
        P = self.P
        c = P.dve(lambda e: e.tensor_scalar(self.s2[:], self.ss[:], 1e-24, None, ALU.max), a)
        self.ssfree = c
        return P.act(lambda e: e.activation(self.s3[:], self.s2[:], ACT.Sqrt), c)

    def inverse(self, d):
        return self.P.dve(lambda e: e.reciprocal(self.rn[:], self.s3[:]), d, self.last)


def layer0(nc, A, C, S):
    with ExitStack() as ctx:
        P = Phase(nc, ctx, "a")
        W, rows = P.sb("W", [128, 3, 128]), P.sb("rows", [128, 3, 128])
        adj = [Buf(C["adj"][i]) for i in range(2)]
        adjch = [[P.chan(f"adj{i}{k}") for k in range(NK)] for i in range(2)]
        xt, xch, xsch = Buf(P.sb("x", [128, NK, 128])), P.chan("x"), P.chan("xs")
        xlch = P.chan("xl")
        hT = [Buf(P.sb(f"hT{i}", [128, N])) for i in range(2)]
        Hr = [Buf(P.sb(f"Hr{i}", [128, NK, 128])) for i in range(2)]
        nh = [Buf(P.sb(f"nh{i}", [128, N], F32R)) for i in range(2)]
        nl = [Buf(P.sb(f"nl{i}", [128, N], F32R)) for i in range(2)]
        tmp = Buf(P.sb("tmp", [128, NK, 128]))
        ew = [Buf(P.sb(f"ew{i}", [128, 512])) for i in range(3)]
        acc = [Buf(P.ps(f"acc{i}", [128, 512])) for i in range(2)]
        cos = [Buf(P.ps(f"cos{i}", [128, 512])) for i in range(2)]
        pp = Buf(P.ps("pp", [128, NK, 128]))
        ln = LayerNorm(P, C)
        rn = RowNorm(P)
        dil = Dilation(P, C)
        ch = P.chan("w")
        P.dma("sp", ch, W[:], A["W"][:, 0:3, :])
        wtok = P.dma("sp", ch, rows[:], A["rows"][0:3, :].partition_broadcast(128))

        units = []
        for u in range(3 * G):
            pi, r = divmod(u, 6)
            units.append((2 * pi + r % 2, r // 2))
        adjtok, later = {}, {}

        def load_adj(g, ks):
            b = adj[g % 2]
            for k in ks:
                adjtok[g, k] = P.dma("sp", adjch[g % 2][k], b.t[:, k, :], A["adjT"][g, blk(k), :], b.free)

        def load_x(g):
            xt.ready = P.dma("sp", xch, flat2(xt.t), A["x"][g], xt.free)

        def transposes(src, tok):
            for k in range(NK):
                t = P.pe(lambda e, k=k: e.transpose(pp.t[:, k, :], src(k), C["ident"][:]), tok, pp.free,
                         sig=(k == NK - 1))
            return t

        def load_ln(g):
            tmp.ready = P.dma("sp", xlch, flat2(tmp.t), A["x"][g], tmp.free)
            tmp.free = []

        def prep_ln(g, src=tmp):
            h, st = hT[g % 2], {}

            def a():
                st["s"] = ln.moments(src.t, src.ready)

            def b():
                st["t"] = src.free = ln.rows(src.t, tmp.t, st["s"], tmp.free)

            def c():
                tt = transposes(lambda k: tmp.t[:, k, :], st["t"])
                tmp.free = [tt]
                h.ready = P.act(lambda e: e.activation(h.t[:], flat2(pp.t), ACT.Relu), tt, h.free)
                pp.free = [h.ready]
            return a, b, c

        def prep_h(u):
            g, i = units[u]
            h, H, n, m = hT[g % 2], Hr[g % 2], nh[g % 2], nl[g % 2]
            st = {}

            def a():
                for k in range(NK):
                    t = P.pe(lambda e, k=k: e.matmul(pp.t[:, k, :], h.t[:, blk(k)], W[:, i, :], start=True, stop=True),
                             h.ready, pp.free, wtok, sig=(k == NK - 1))
                h.free = [t]
                st["t"] = t

            def b():
                H.ready = P.dve(lambda e: e.tensor_tensor(
                    H.t[:], pp.t[:], rows[:, i, :].unsqueeze(1).to_broadcast([128, NK, 128]), ALU.add),
                    st["t"], H.free, wtok)
                pp.free = [H.ready]
                st["sq"] = rn.sums(tmp.t, H.t, [H.ready] * NK, tmp.free)

            def c():
                st["d"] = rn.root(st["sq"])

            def d():
                r = rn.inverse(st["d"])
                st["v"] = rn.last = P.dve(lambda e: e.tensor_tensor(tmp.t[:], H.t[:], bc(rn.rn[:], 128), ALU.mult),
                                          r, H.ready, st["sq"])

            def f():
                tt = transposes(lambda k: tmp.t[:, k, :], st["v"])
                tmp.free = [tt]
                st["tt"] = tt
                n.ready = P.act(lambda e: e.activation(n.t[:], flat2(pp.t), ACT.Copy), tt, n.free)

            def o():
                m.ready = P.dve(lambda e: e.tensor_tensor(m.t[:], flat2(pp.t), n.t[:].bitcast(F32), ALU.subtract),
                                n.ready, m.free)
                pp.free = [m.ready]
            return a, b, c, d, f, o

        def evac(u, j):
            g, i = units[u]
            h = hT[g % 2]
            f = ACT.Relu if i < 2 else ACT.Copy
            t = P.act(lambda e: e.activation(h.t[:, j * 512:j * 512 + 512], acc[j].t[:], f), acc[j].ready, h.free)
            acc[j].free = [t]
            h.ready = t

        def post(u):
            g, i = units[u]
            h, st = hT[g % 2], {}

            def a():
                st["t"] = transposes(lambda k: h.t[:, blk(k)], h.ready)
                h.free = [st["t"]]

            def b():
                s = P.dve(lambda e: e.tensor_tensor(xt.t[:], pp.t[:], xt.t[:], ALU.add), st["t"], xt.ready)
                pp.free = [s]
                xt.free = [P.dma("sp", xsch, S["x1"][g], flat2(xt.t), s)]
            return a, b

        def do_cos(u, k, j):
            g, i = units[u]
            n, m, a, c = nh[g % 2], nl[g % 2], adj[g % 2], cos[j]
            parts = [(n, n), (n, m), (m, n)]
            for x, (l, r) in enumerate(parts):
                t = P.pe(lambda e, l=l, r=r, x=x: e.matmul(c.t[:], l.t[:, blk(k)], r.t[:, j * 512:j * 512 + 512],
                                                           start=(x == 0), stop=(x == 2)),
                         n.ready, m.ready, c.free, sig=(x == 2))
            w = ew[(2 * (u * NK + k) + j) % 3]
            v = P.dve(lambda e: e.tensor_tensor(w.t[:], a.t[:, k, j * 512:j * 512 + 512], c.t[:], ALU.mult),
                      t, w.free, adjtok[g, k])
            c.free = [v]
            w.ready = v
            if k == NK - 1 and j == 1:
                n.free = m.free = [t]
                if i == 2:
                    a.free = [v]

        def do_agg(u, k, j):
            g, i = units[u]
            H, w = Hr[g % 2], ew[(2 * (u * NK + k) + j) % 3]
            t = P.pe(lambda e: e.matmul(acc[j].t[:], H.t[:, k, :], w.t[:], start=(k == 0), stop=(k == NK - 1)),
                     w.ready, H.ready, acc[j].free if k == 0 else None)
            w.free = [t]
            acc[j].ready = t
            if k == NK - 1 and j == 1:
                H.free = [t]

        load_ln(0)
        load_x(1)
        load_adj(0, range(NK))
        for f in (*prep_ln(0), *prep_h(0)):
            f()
        load_adj(1, range(NK))
        fills = [(i, k, h, A["adjT"][i]) for k in range(NK) for i in range(Q) for h in range(2)]
        for f in fills[:2 * Q]:
            dil.fill(*f)
        fills = fills[2 * Q:]
        stages = dil.stages(A, S, fills)
        lead, total, done, late = 12, 6 * G * NK, 0, []
        at, width = 0.0, sum(w for f, w in stages)
        steps = [(u, k) for u in range(3 * G) for k in range(NK)]

        agenda = {}

        def plan(pieces, halves):
            for f, n in zip(pieces, halves):
                agenda.setdefault(n, []).append(f)

        def flush():
            while late:
                late.pop(0)()

        do_cos(0, 0, 0)
        do_cos(0, 0, 1)
        for s, (u, k) in enumerate(steps):
            ends = u >= 1 and units[u - 1][1] == 2
            g2, i2 = units[u + 1] if u + 1 < 3 * G else (None, None)
            g3, i3 = units[u + 2] if u + 2 < 3 * G else (None, None)
            for j in range(2):
                half, here = 2 * s + j, 2 * k + j
                if ends and here == 0:
                    plan(post(u - 1), (1, 2))
                if ends and units[u - 1][0] + 2 < G and here < NK:
                    load_adj(units[u - 1][0] + 2, [here])
                if i2 == 0 and here == 0:
                    plan(prep_ln(g2, xt if u == 0 else tmp), (0, 2, 4))
                    plan(prep_h(u + 1), (5, 6, 8, 9, 11, 12))
                elif i2 is not None and here == 0:
                    plan(prep_h(u + 1), (4, 5, 7, 8, 10, 11))
                if i3 == 0 and here == 14:
                    load_ln(g3)
                if units[u][1] == 2 and here == 10:
                    load_x(units[u][0])
                if s + 1 < len(steps):
                    do_cos(*steps[s + 1], j)
                do_agg(u, k, j)
                for f in agenda.pop(here, []):
                    f()
                flush()
                if k == NK - 1:
                    evac(u, j)
                if half < lead and fills and half % 2:
                    dil.fill(*fills.pop(0))
                while done < len(stages) and at * (total - lead) < (half + 1 - lead) * width:
                    flush()
                    late += stages[done][0]() or []
                    at += stages[done][1]
                    done += 1
        flush()
        for f in post(3 * G - 1):
            f()
        for f, w in stages[done:]:
            for piece in f() or []:
                piece()
        P.run()


class Dilation:

    def __init__(self, P, C):
        self.C = C
        self.AT = [Buf(P.sb(f"AT{i}", [128, NK, N], FP8)) for i in range(Q)]
        self.R = [Buf(P.sb(f"R{i}", [128, NK, N], FP8)) for i in range(Q)]
        self.ats = [Buf(P.sb(f"ats{i}", [128, 4, 128])) for i in range(2)]
        self.af = [Buf(P.sb(f"af{i}", [128, 512])) for i in range(3)]
        self.Ab = [Buf(P.sb(f"Ab{i}", [128, N], FP8)) for i in range(2 * Q)]
        self.Au = P.sb("Au", [128, 128], FP8)
        self.X = [P.sb(f"X{i}", [128, 128], FP8) for i in range(Q)]
        self.Sd = [[P.sb(f"Sd{i}{j}", [128, 128], FP8) for j in range(2)] for i in range(Q)]
        self.v8 = P.sb("v8", [128, 128], FP8)
        self.base = P.sb("base", [128, 2, 2, 2])
        self.cnt = P.sb("cnt", [128, 2, 2])
        self.b1 = P.sb("b1", [128, Q])
        self.vr = P.sb("vr", [128, Q, 128], F16)
        self.v = [Buf(P.sb(f"v{i}", [128, 512], F16)) for i in range(3)]
        self.kp = [Buf(P.sb(f"kp{i}", [128, N], FP8)) for i in range(2)]
        self.small = {n: P.sb(f"sm_{n}", [128, Q]) for n in ("t", "sf", "sc", "va", "h", "b", "c", "b2")}
        self.D = P.ps("D", [128, 2, 512])
        self.bank = [Buf(self.D[:, b, :]) for b in range(2)]
        self.attach(P)

    def attach(self, P):
        self.P = P
        self.atsch = [P.chan(f"ats{i}") for i in range(2)]
        self.afch = [P.chan(f"af{i}") for i in range(3)]
        self.kpch = [P.chan(f"kp{i}") for i in range(2)]
        for b in (*self.AT, *self.R, *self.ats, *self.af, *self.Ab, *self.v, *self.kp, *self.bank):
            b.free, b.ready = [], None
        self.nv = self.nb = self.nk = self.nf = 0
        self.smallfree, self.vrfree = [], []
        self.b1tok, self.b1free = None, [None] * Q
        self.attok = {}
        self.atfree = {}
        self.basetok = self.autok = self.v8tok = self.ruletok = None
        self.xtok, self.xfree = [None] * Q, [None] * Q
        self.sdtok = [[None, None] for _ in range(Q)]
        self.sdfree = [[None, None] for _ in range(Q)]
        self.ranktok = [None] * Q
        self.vrtok = [None] * Q

    def fill(self, i, k, h, src):
        P, AT, a = self.P, self.AT[i], self.ats[h]
        l = P.dma("sp", self.atsch[h], a.t[:], src[h * 512:h * 512 + 512, blk(k)].rearrange("(q p) n -> p q n", p=128), a.free)
        t = P.pool(lambda e: e.tensor_scalar(AT.t[:, 4 * h:4 * h + 4, blk(k)].bitcast(U8), a.t[:], 0.0, ONE8,
                                             ALU.is_gt, ALU.mult), l, self.atfree.get((i, k)))
        a.free = [t]
        self.attok[i, k] = t

    def rowload(self, i, k, j, src):
        b, f, h = self.Ab[Q * (k % 2) + i], self.nf % 3, slice(j * 512, j * 512 + 512)
        a = self.af[f]
        self.nf += 1
        l = self.P.dma("sp", self.afch[f], a.t[:], src[:, h], a.free)

        def sign():
            b.ready = self.P.act(lambda e: e.activation(b.t[:, h], a.t[:], ACT.Sign, saturate=False), l, b.free)
            a.free = [b.ready]
        return sign

    def rank(self, i):
        return self.D[:, i // 2, (i % 2) * 144:(i % 2) * 144 + 144]

    def count(self, i, src, *waits):
        b = self.bank[i // 2]
        t = self.P.pe(lambda e: e.matmul(self.rank(i)[:, 0:129], src, self.C["U2"][:, 0:129], start=True, stop=True),
                      waits, b.free)
        self.ranktok[i] = t
        return t

    def start(self, i, k):
        P, C = self.P, self.C
        self.k = k
        AT, R, ab = self.AT[i], self.R[i], self.Ab[Q * (k % 2) + i]
        low = at = self.attok.get((i, k))
        if k:
            low = P.dve(lambda e: e.tensor_tensor(AT.t[:, 0:k, blk(k)], AT.t[:, 0:k, blk(k)], R.t[:, 0:k, blk(k)],
                                                  ALU.is_gt, saturate=False), at, R.ready)
        self.attok[i, k] = [at, low]
        au = P.dve(lambda e: e.scalar_tensor_tensor(self.Au[:], ab.t[:, blk(k)], 0.0, C["tri"][:], ALU.max, ALU.mult,
                                                    saturate=False), ab.ready, self.autok)
        self.xtok[i] = self.autok = P.dve(lambda e: e.scalar_tensor_tensor(
            self.X[i][:], AT.t[:, k, blk(k)], 2.0, self.Au[:], ALU.mult, ALU.subtract, saturate=False), at, au, self.xfree[i])
        others = [q for q in range(NK) if q != k]

        def counts():
            for q in others:
                P.pe(lambda e, q=q: e.matmul(self.rank(i)[:, 132:134], AT.t[:, q, blk(k)],
                                             (C["two1"] if q < k else C["zero1"])[:], start=(q == others[0]),
                                             stop=(q == others[-1])),
                     low, at, self.bank[i // 2].free, sig=False)
            self.count(i, AT.t[:, k, blk(k)], at)
        return [counts]

    def rule(self, mv, first):
        P, C, s = self.P, self.C, self.small
        num, sf, flat4 = self.cnt, s["sf"], self.cnt[:].rearrange("p b i -> p (b i)")
        D = self.D[:, :, 0:288].rearrange("p b (i c) -> p b i c", c=144)
        base = lambda c: self.base[:].rearrange("p b i c -> p (b i) c")[:, :, c]
        if first:
            self.basetok = P.dve(lambda e: e.tensor_copy(self.base[:], D[:, :, :, 132:134]), self.ranktok, self.smallfree)
        n = P.dve(lambda e: e.tensor_tensor(num[:], D[:, :, :, 128], self.base[:, :, :, 1], ALU.add), self.ranktok,
                  self.basetok, self.smallfree)
        a = P.dve(lambda e: e.tensor_scalar(s["t"][:], flat4, 0.5, 0.5, ALU.add, ALU.mult), n)
        c = P.dve(lambda e: e.scalar_tensor_tensor(s["sc"][:], flat4, 10.5, mv, ALU.is_gt, ALU.mult), n)
        d = P.dve(lambda e: e.scalar_tensor_tensor(s["va"][:], flat4, 1.5, mv, ALU.is_gt, ALU.mult), n)
        b = P.dve(lambda e: e.tensor_scalar(sf[:], s["t"][:], MAGIC, MAGIC, ALU.add, ALU.subtract), a)
        q = P.dve(lambda e: e.tensor_tensor(s["c"][:], s["sc"][:], base(0), ALU.mult), c)
        h = P.dve(lambda e: e.scalar_tensor_tensor(s["h"][:], s["sc"][:], -4.0, s["va"][:], ALU.mult, ALU.add), c, d)
        p = P.dve(lambda e: e.tensor_tensor(s["b"][:], sf[:], s["h"][:], ALU.mult), h, b)
        b2 = P.dve(lambda e: e.tensor_tensor(s["b2"][:], s["b"][:], s["c"][:], ALU.add), p, q)
        self.ruletok = [b2, p]
        self.smallfree = []
        self.bank[0].free, self.bank[1].free = [n], [n]
        for i in range(Q):
            t = P.act(lambda e, i=i: e.activation(self.vr[:, i, :], self.rank(i)[:, 0:128], ACT.Abs,
                                                  bias=s["b2"][:, i:i + 1], scale=s["sc"][:, i:i + 1]),
                      self.ranktok, n, self.ruletok, self.vrfree)
            self.vrtok[i] = t
            self.bank[i // 2].free.append(t)
            self.smallfree.append(t)
        self.vrfree = []

    def drop(self, r, last):
        P, s = self.P, self.small
        for i in range(Q):
            new = self.Sd[i][(r + 1) % 2]
            x = P.dve(lambda e, i=i, new=new: e.scalar_tensor_tensor(
                new[:], self.vr[:, i, :], s["sf"][:, i:i + 1], self.X[i][:], ALU.is_equal, ALU.is_lt, saturate=False),
                self.vrtok[i], self.xtok[i], self.sdfree[i][(r + 1) % 2])
            self.sdtok[i][(r + 1) % 2] = x
            self.xfree[i] = x
            self.vrfree.append(x)
            self.smallfree.append(x)

        def counts():
            for i in range(Q):
                self.sdfree[i][(r + 1) % 2] = self.count(i, self.Sd[i][(r + 1) % 2][:], self.sdtok[i][(r + 1) % 2])
        return [] if last else [counts]

    def settled(self, i, r, col):
        self.v8tok = self.P.dve(lambda e: e.scalar_tensor_tensor(
            self.v8[:], self.Sd[i][0][:], 1.0, self.Sd[i][1][:], ALU.mult, ALU.not_equal, accum_out=col, saturate=False),
            self.sdtok[i], self.v8tok)

    def wide(self, i, j, r):
        P, C, s, k = self.P, self.C, self.small, self.k
        AT, R, ab = self.AT[i], self.R[i], self.Ab[Q * (k % 2) + i]
        w = self.bank[self.nb % 2]
        v = self.v[self.nv % 3]
        self.nb += 1
        self.nv += 1
        qs = range(4 * j, 4 * j + 4)
        bias = self.b1[:, i:i + 1] if j else s["b"][:, i:i + 1]
        sd = self.Sd[i][(r + 1) % 2]
        for q in qs:
            lo = max(q * 128, j * 512)
            src = sd[:] if q == k else AT.t[:, q, blk(k)]
            t = P.pe(lambda e, q=q, lo=lo, src=src: e.matmul(
                w.t[:, lo - j * 512:512], src, C["UL"][:, lo - q * 128:j * 512 + 512 - q * 128],
                start=(q == qs[0]), stop=(q == qs[-1]), skip_group_check=True),
                w.free, self.sdtok[i][(r + 1) % 2], self.attok.get((i, k)), sig=(q == qs[-1]))
        a = P.act(lambda e: e.activation(v.t[:], w.t[:], ACT.Abs, bias=bias, scale=s["sc"][:, i:i + 1]),
                  t, self.ruletok, v.free, self.b1tok)
        w.free = [a]
        if j == 0:
            self.b1tok = P.act(lambda e: e.activation(self.b1[:, i:i + 1], w.t[:, 511:512], ACT.Identity,
                                                      bias=s["b"][:, i:i + 1], scale=s["sc"][:, i:i + 1]),
                               t, self.ruletok, self.b1free[i])
            w.free.append(self.b1tok)
            self.smallfree.append(self.b1tok)
        else:
            self.b1free[i] = a
        if k // 4 == j:
            self.sdfree[i][(r + 1) % 2] = t
        self.atfree[i, k] = t

        def finish():
            x = P.dve(lambda e: e.scalar_tensor_tensor(
                R.t[:, k, j * 512:j * 512 + 512], v.t[:], s["sf"][:, i:i + 1], ab.t[:, j * 512:j * 512 + 512],
                ALU.not_equal, ALU.is_lt, saturate=False), a, ab.ready, R.free)
            v.free = [x]
            ab.free = [x, self.xtok[i]]
            R.ready = x
            self.smallfree += [a, x]
        return finish

    def mask(self, i, q, dst):
        P, C, R = self.P, self.C, self.R[i]
        kp, ch = self.kp[self.nk % 2], self.kpch[self.nk % 2]
        self.nk += 1
        turned = []
        for j in range(2):
            w = self.bank[self.nb % 2]
            self.nb += 1
            for b in range(4):
                t = P.pe(lambda e, b=b, w=w, j=j: e.matmul(w.t[:, blk(b)], R.t[:, 4 * j + b, blk(q)], C["ident8"][:],
                                                           start=True, stop=True), R.ready, w.free, sig=(b == 3))
            turned.append((w, t))
        free = kp.free

        def finish():
            for j, (w, t) in enumerate(turned):
                a = P.dve(lambda e, w=w, j=j: e.scalar_tensor_tensor(
                    kp.t[:, j * 512:j * 512 + 512], w.t[:], 0.5, R.t[:, q, j * 512:j * 512 + 512], ALU.is_lt, ALU.is_gt,
                    saturate=False), t, free)
                w.free = [a]
            if q == NK - 1:
                R.free = [t, a]
            kp.free = [P.dma("sp", ch, dst, kp.t[:].bitcast(U8), a)]
        return finish

    def stages(self, A, S, fills):
        C, out, pend, signs = self.C, [], [], []
        blocks = [(quad, k) for quad in range(G // Q) for k in range(NK)]
        mv = C["mv"][:].rearrange("p (g k) -> p g k", k=NK)
        todo = []

        def rowload(g0, i, k, j):
            signs.append(self.rowload(i, k, j, A["adj"][g0 + i, blk(k), :]))

        def flush():
            while pend:
                pend.pop(0)()

        def add(f, width=1.0):
            def piece(load=todo.pop(0) if todo else None, turn=len(out)):
                if fills and turn % 2:
                    self.fill(*fills.pop(0))
                if load:
                    rowload(*load)
                if signs and (len(signs) > 2 or not load):
                    signs.pop(0)()
                return f()
            out.append((piece, width))

        def wide(i, k, r):
            for j in range(2):
                f = self.wide(i, j, r)
                if len(pend) > 1:
                    pend.pop(0)()
                pend.append(f)

        def start(i, k):
            flush()
            return self.start(i, k)

        def check(g0, k, r):
            for i in range(Q):
                c = (g0 + i) * NK + k
                self.settled(i, r, C["flags"][:, c:c + 1])

        def refill(g0, i, k):
            if g0 + Q < G:
                fills.extend((i, k, h, A["adjT"][g0 + Q + i]) for h in range(2))

        def masks(g0, i, q):
            f = self.mask(i, q, S["keep"][g0 + i, q])
            return f()

        for i in range(Q):
            for j in range(2):
                add(lambda i=i, j=j: rowload(0, i, 0, j))
        add(lambda: None)
        add(lambda: None)
        add(lambda: None)
        for n, (quad, k) in enumerate(blocks):
            g0, K = quad * Q, ROUNDS[k]
            if n + 1 < len(blocks):
                todo.extend((blocks[n + 1][0] * Q, i, blocks[n + 1][1], j) for i in range(Q) for j in range(2))
            for i in range(Q):
                add(lambda i=i, k=k: start(i, k), 1)
            for r in range(K):
                add(lambda r=r, k=k, g0=g0: self.rule(mv[:, g0:g0 + Q, k], r == 0), 0.9)
                add(lambda r=r, K=K: self.drop(r, r == K - 1), 0.9)
            add(lambda g0=g0, k=k, K=K: check(g0, k, K - 1), 0.5)
            for i in range(Q):
                add(lambda g0=g0, i=i, k=k, K=K: (wide(i, k, K - 1), refill(g0, i, k)) and None, 1.15)
            if k == NK - 1:
                add(flush)
                for i in range(Q):
                    for q in range(NK):
                        add(lambda i=i, q=q, g0=g0: masks(g0, i, q), 1)
        return out


def changed(nc, C):
    with ExitStack() as ctx:
        P = Phase(nc, ctx, "n")
        r, ps = P.sb("r", [128, 1]), P.ps("ps", [128, 1])
        a = P.dve(lambda e: e.tensor_reduce(r[:], C["flags"][:], AXX, ALU.add))
        ones = P.sb("ones", [128, 128])
        o = P.dve(lambda e: e.memset(ones[:], 1.0))
        b = P.pe(lambda e: e.matmul(ps[:], ones[:], r[:], start=True, stop=True), a, o)
        P.dve(lambda e: e.tensor_copy(C["flag"][:], ps[:]), b)
        P.run()
    return nc.values_load(C["flag"][0:1, 0:1], min_val=0, max_val=128 * 128 * 128)


def dilate_all(nc, A, C, S):
    with ExitStack() as ctx:
        M = Phase(nc, ctx, "g")
        mi, mf, mv = M.sb("mi", [128, Q, NK], I32), M.sb("mf", [128, Q, NK]), M.sb("mv", [128, Q, NK])
        dil = Dilation(M, C)
        M.chan("m")

        def stage(fill):
            P = Phase(nc, ctx, "g", M.sems)
            dil.attach(P)
            fill(P)
            P.run()
            for s in P.sems.values():
                nc.sync.sem_clear(s)
            nc.all_engine_barrier()

        with nc.Fori(0, G // Q) as quad:
            def graph(t, i):
                return t[bass.ds(quad * Q + i, 1)]

            def load(P):
                t = P.dma("sp", P.chan("m"), mi[:].rearrange("p i k -> p (i k)"), A["mask"][:, bass.ds(quad * Q * NK, Q * NK)])
                a = P.dve(lambda e: e.tensor_copy(mf[:], mi[:]), t)
                P.dve(lambda e: e.tensor_scalar(mv[:], mf[:], 0.0, None, ALU.not_equal), a)
                for k in range(NK):
                    for i in range(Q):
                        for h in range(2):
                            dil.fill(i, k, h, graph(A["adjT"], i).rearrange("o n m -> (o n) m"))

            def start(k):
                def fill(P):
                    for i in range(Q):
                        for j in range(2):
                            dil.rowload(i, k, j, graph(A["adj"], i).rearrange("o n m -> (o n) m")[blk(k), :])()
                    for i in range(Q):
                        dil.start(i, k)[0]()
                    dil.rule(mv[:, :, k], True)
                    dil.drop(0, False)[0]()
                return fill

            def again(k):
                def fill(P):
                    dil.rule(mv[:, :, k], False)
                    dil.drop(0, False)[0]()
                return fill

            def wide(P):
                for i in range(Q):
                    for j in range(2):
                        dil.wide(i, j, 0)()

            def masks(i, q):
                def fill(P):
                    dil.mask(i, q, graph(S["keep"], i)[:, q].rearrange("o p n -> (o p) n"))()
                return fill

            stage(load)
            for k in range(NK):
                stage(start(k))
                with nc.Fori(0, 127):
                    stage(again(k))
                stage(wide)
            for i in range(Q):
                for q in range(NK):
                    stage(masks(i, q))


ORDER = [G - 2, G - 1] + list(range(G - 2))


NONE = [None] * NK


class Sage:

    def __init__(self, P, A, C, S, kps, on_dve=NK):
        self.P, self.A, self.C, self.S, self.on_dve = P, A, C, S, on_dve
        self.adj = [Buf(t) for t in C["adj"]]
        self.adjch = [[P.chan(f"adj{i}{c}") for c in range(4)] for i in range(3)]
        self.kp = [Buf(P.sb(f"kp{i}", [128, NK, N], FP8)) for i in range(kps)]
        self.kpch = [P.chan(f"kp{i}") for i in range(kps)]
        self.acc = [Buf(P.ps(f"acc{i}", [128, 512])) for i in range(2)]
        self.masked = {}
        self.kptok = {}
        self.adjtok = {}

    def load_keep(self, n):
        P, c = self.P, self.kp[n % len(self.kp)]
        self.kptok[n] = P.dma("sp", self.kpch[n % len(self.kp)], c.t[:].bitcast(U8),
                              self.S["keep"][ORDER[n]].rearrange("k p n -> p k n"), c.free)

    def load_adj(self, n):
        P, b, src = self.P, self.adj[n % 3], self.A["adjT"][ORDER[n]].rearrange("(k p) n -> p k n", p=128)
        for c in range(4):
            t = P.dma("sp", self.adjch[n % 3][c], b.t[:, 2 * c:2 * c + 2, :], src[:, 2 * c:2 * c + 2, :], b.free)
            self.adjtok[n, 2 * c] = self.adjtok[n, 2 * c + 1] = t

    def mask(self, n):
        P = self.P
        b, c = self.adj[n % 3], self.kp[n % len(self.kp)]
        self.masked[n] = [(P.dve if q < self.on_dve else P.pool)(
            lambda e, q=q: e.tensor_tensor(b.t[:, q, :], b.t[:, q, :], c.t[:, q, :], ALU.mult),
            self.kptok[n], self.adjtok.get((n, q))) for q in range(NK)]
        c.free = self.masked[n]

    def agg(self, n, rows, tok, js=(0, 1)):
        P, b = self.P, self.adj[n % 3]
        for j in js:
            for q in range(NK):
                t = P.pe(lambda e, q=q, j=j: e.matmul(self.acc[j].t[:], rows[:, q, :], b.t[:, q, j * 512:j * 512 + 512],
                                                      start=(q == 0), stop=(q == NK - 1)),
                         tok, self.masked.get(n, NONE)[q], self.acc[j].free if q == 0 else None, sig=(q == NK - 1))
            self.acc[j].ready = t
        return t

    def evac(self, dst, free, js=(0, 1)):
        P = self.P
        for j in js:
            t = P.act(lambda e, j=j: e.activation(dst[:, j * 512:j * 512 + 512], self.acc[j].t[:], ACT.Copy),
                      self.acc[j].ready, free)
            self.acc[j].free = [t]
        return t


def flat2(t):
    return t[:].rearrange("p k d -> p (k d)")


class Dense:

    def __init__(self, P, C, transposed, order):
        self.P, self.C, self.order = P, C, order
        self.p1 = Buf(P.ps("p1", [128, NK, 128]))
        self.p2 = Buf(P.ps("p2", [128, NK, 128]))
        self.o = [Buf(P.sb(f"o{i}", [128, NK, 128])) for i in range(2)]
        self.z = [Buf(P.sb(f"z{i}", [128, NK, 128])) for i in range(2)]
        self.zT = transposed
        self.rn = RowNorm(P)
        self.rm = P.sb("rm", [128, NK])
        self.rmfree = None

    def mm(self, dst, lhsT, rhs, *waits):
        P = self.P
        for k in range(NK):
            t = P.pe(lambda e, k=k: e.matmul(dst.t[:, k, :], lhsT[:, blk(k)], rhs, start=True, stop=True),
                     waits, dst.free, sig=(k == NK - 1))
        return t

    def products(self, aggT, hT, Wr, Wx, waits, second_first=False):
        if second_first:
            self.b = self.mm(self.p2, hT, Wx, waits)
        self.a = self.mm(self.p1, aggT, Wr, waits)
        if not second_first:
            self.b = self.mm(self.p2, hT, Wx, waits)
        return self.a, self.b

    def rows(self, n, bias, rank1=None, between=None):
        P, C, o, z, g = self.P, self.C, self.o[n % 2], self.z[n % 2], self.order[n]
        c = P.dve(lambda e: e.tensor_tensor(o.t[:], self.p2.t[:], bias.unsqueeze(1).to_broadcast([128, NK, 128]),
                                            ALU.add), self.b, o.free)
        self.p2.free = [c]
        f = [P.dve(lambda e, k=k: e.scalar_tensor_tensor(o.t[:, k, :], self.p1.t[:, k, :], C["rdeg"][:, g, k:k + 1],
                                                         o.t[:, k, :], ALU.mult, ALU.add), self.a, c) for k in range(NK)]
        self.p1.free = [f[-1]]
        if rank1 is not None:
            f = [P.dve(lambda e, k=k: e.scalar_tensor_tensor(o.t[:, k, :], rank1, C["rho"][:, g, k:k + 1],
                                                             o.t[:, k, :], ALU.mult, ALU.add), f[k]) for k in range(NK)]
        if between:
            between()
        r, s = self.rn(z.t, o.t, f, z.free)
        m = P.dve(lambda e: e.tensor_tensor(self.rm[:], self.rn.rn[:], col8(C["mf"], g), ALU.mult), r, self.rmfree)
        self.rn.last = m
        z.ready = [P.act(lambda e, k=k: e.activation(z.t[:, k, :], o.t[:, k, :], ACT.Relu, scale=self.rm[:, k:k + 1]),
                         m, f[k], s[k], z.free) for k in range(NK)]
        o.free = self.rmfree = [z.ready[-1]]
        z.free = []

    def turn(self, n, stats):
        P, z, zT = self.P, self.z[n % 2], self.zT(n)
        for k in range(NK):
            t = P.pe(lambda e, k=k: e.transpose(self.p2.t[:, k, :], z.t[:, k, :], self.C["ident"][:]), z.ready,
                     self.p2.free, sig=(k == NK - 1))
        z.free.append(t)
        zT.ready = P.act(lambda e: e.activation(zT.t[:], flat2(self.p2.t), ACT.Copy), t, zT.free)
        self.p2.free = [zT.ready]
        zT.free = [P.dve(lambda e, j=j: e.bn_stats(stats[:, 2 * n + j, :], zT.t[:, j * 512:j * 512 + 512]), zT.ready)
                   for j in range(2)]


def pair(bufs):
    return lambda g: bufs[g % 2]


def layer1_first(nc, A, C, S):
    with ExitStack() as ctx:
        P = Phase(nc, ctx, "b")
        sg = Sage(P, A, C, S, 2)
        dn = Dense(P, C, pair([Buf(P.sb(f"zT{i}", [128, N])) for i in range(2)]), ORDER)
        ln = LayerNorm(P, C)
        stats = nc_stats(P, C)
        x = [Buf(P.sb(f"x{i}", [128, NK, 128])) for i in range(2)]
        xch = [P.chan(f"x{i}") for i in range(2)]
        h = [Buf(P.sb(f"h{i}", [128, NK, 128])) for i in range(2)]
        hT, aT = Buf(P.sb("hT", [128, N])), Buf(P.sb("aT", [128, N]))
        a1 = Buf(P.sb("a1", [128, N]))
        a1ch = P.chan("a1")
        zch = [P.chan(f"z{i}") for i in range(2)]
        dsums = [Buf(P.sb(f"dsum{i}", [128, N])) for i in range(2)]
        dg = P.sb("dg", [128, NK])
        dp = P.ps("dp", [128, NK])
        pt = dn.p1
        xtok, degfree = {}, []

        def load(n):
            xtok[n] = P.dma("sp", xch[n % 2], flat2(x[n % 2].t), S["x1"][ORDER[n]], x[n % 2].free)
            sg.load_keep(n)
            if n > 1:
                sg.load_adj(n)

        def prep(n):
            xb, hb = x[n % 2], h[n % 2]
            t = ln(xb.t, xb.t, xtok[n], None)
            hb.ready = P.act(lambda e: e.activation(hb.t[:], xb.t[:], ACT.Relu), t, hb.free)
            xb.free = [hb.ready]
            hb.free = []
            sg.mask(n)
            b = sg.adj[n % 3]
            m, dsum = sg.masked[n], dsums[n % 2]
            d = P.pool(lambda e: e.tensor_tensor(dsum.t[:], b.t[:, 0, :], b.t[:, 1, :], ALU.add), m[0], m[1], dsum.free)
            for q in range(2, NK):
                d = P.pool(lambda e, q=q: e.tensor_tensor(dsum.t[:], dsum.t[:], b.t[:, q, :], ALU.add), d, m[q])
            b.pool = d
            dsum.ready = d

        def degree(n):
            g, dsum = ORDER[n], dsums[n % 2]
            for k in range(NK):
                t = P.pe(lambda e, k=k: e.matmul(dp[:, k:k + 1], dsum.t[:, blk(k)], C["onesf"][:, 0:1], start=True,
                                                 stop=True), dsum.ready, degfree, sig=(k == NK - 1))
            dsum.free = [t]
            a = P.dve(lambda e: e.tensor_scalar(dg[:], dp[:], 1.0, None, ALU.max), t, degfree)
            b = P.dve(lambda e: e.reciprocal(C["rdeg"][:, g, :], dg[:]), a)
            c = P.dve(lambda e: e.tensor_tensor(C["rho"][:, g, :], dp[:], C["rdeg"][:, g, :], ALU.mult), b)
            degfree[:] = [b, c]

        load(0)
        load(1)
        prep(0)
        load(2)
        for n in range(G + 1):
            if n < G:
                hb = h[n % 2]
                t = sg.agg(n, hb.t, hb.ready)
                hb.free.append(t)
                for k in range(NK):
                    t = P.pe(lambda e, k=k, hb=hb: e.transpose(pt.t[:, k, :], hb.t[:, k, :], C["ident"][:]), hb.ready,
                             pt.free, sig=(k == NK - 1))
                hb.free.append(t)
                aT.ready = sg.evac(aT.t, aT.free)
                hT.ready = P.act(lambda e: e.activation(hT.t[:], flat2(pt.t), ACT.Copy), t, hT.free)
                pt.free = [hT.ready]
            if n + 1 < G:
                prep(n + 1)
            if n:
                dn.turn(n - 1, stats)
                z, zT, b = dn.z[(n - 1) % 2], dn.zT(n - 1), sg.adj[(n - 1) % 3]
                zT.free.append(P.dma("sp", zch[(n - 1) % 2], S["z1"][ORDER[n - 1]], zT.t[:], zT.ready))
                t = sg.agg(n - 1, z.t, z.ready)
                z.free.append(t)
                b.free = [t, b.pool]
                e = sg.evac(a1.t, a1.free)
                a1.free = [P.dma("sp", a1ch, S["ag1"][ORDER[n - 1]], a1.t[:], e)]
                if n + 2 < G:
                    load(n + 2)
            if n < G:
                degree(n)
                a, b = dn.products(aT.t, hT.t, C["W"][:, 3, :], C["W"][:, 4, :], [aT.ready, hT.ready])
                aT.free, hT.free = [a], [b]
                dn.rows(n, C["rows"][:, 3, :])
        fold(P, C, stats, 1, st_all(P, dn))
        P.run()


def nc_stats(P, C):
    return P.sb("stats", [128, 2 * G, 6])


def st_all(P, dn):
    return [(P.lanes["dve"].sem, P.lanes["dve"].count)]


def fold(P, C, stats, l, waits):
    ag = P.sb("ag", [128, 2])
    sd = P.sb("bsd", [128, 1])
    rs = P.sb("brs", [128, 1])
    ms = P.sb("bms", [128, 1])
    tb = P.sb("btb", [128, 128])
    pv = P.ps("pv", [128, 128])
    s, t, w = C["s"][:, l - 1:l], C["t"][:, l - 1:l], 3 + 2 * l
    a = P.dve(lambda e: e.bn_aggr(ag[:], stats[:].rearrange("p a b -> p (a b)")), waits)
    b = P.act(lambda e: e.activation(sd[:], ag[:, 1:2], ACT.Sqrt, bias=C["eps"][:, 0:1]), a)
    c = P.dve(lambda e: e.reciprocal(rs[:], sd[:]), b)
    d = P.dve(lambda e: e.tensor_tensor(s, rs[:], C["cols"][:, 2 * (l - 1):2 * l - 1], ALU.mult), c)
    f = P.dve(lambda e: e.tensor_tensor(ms[:], ag[:, 0:1], s, ALU.mult), d)
    h = P.dve(lambda e: e.tensor_tensor(t, C["cols"][:, 2 * l - 1:2 * l], ms[:], ALU.subtract), f)
    if l < 3:
        k = P.dve(lambda e: e.tensor_scalar(tb[:], C["onesf"][:], t, None, ALU.mult), h)
        m = P.pe(lambda e: e.matmul(pv[:], tb[:], C["W"][:, w, :], start=True, stop=True), k)
        P.dve(lambda e: e.tensor_copy(C["rows"][:, 6, :], pv[:]), m)
        P.dve(lambda e: e.tensor_scalar(C["W"][:, w, :], C["W"][:, w, :], s, None, ALU.mult), m, d)


def affine(P, C, l, z, *waits, pool=False):
    if pool:
        return P.pool(lambda e: e.tensor_scalar(z, z, C["s"][:, l - 1:l], C["t"][:, l - 1:l], ALU.mult, ALU.add), *waits)
    return P.act(lambda e: e.activation(z, z, ACT.Identity, bias=C["t"][:, l - 1:l], scale=C["s"][:, l - 1:l]), *waits)


def layer1_next(nc, A, C, S, l):
    with ExitStack() as ctx:
        P = Phase(nc, ctx, f"c{l}")
        sums, nb = l == 2, 3
        order = ORDER if sums else list(range(G))
        run = list(range(G))[::-1] if sums else list(range(G))
        sg = Sage(P, A, C, S, 3, 4) if sums else None
        stats = nc_stats(P, C)
        if sums:
            dn = Dense(P, C, pair([Buf(P.sb(f"zT{i}", [128, N])) for i in range(2)]), order)
        else:
            z3 = [Buf(t) for t in C["z3"]]
            dn = Dense(P, C, lambda n: z3[n], order)
            yy = Buf(P.sb("yy", [128, NK, 128]))
            py = Buf(P.ps("py", [128, NK, 128]))
            yi, yich = [Buf(P.sb(f"yi{i}", [128, N])) for i in range(2)], [P.chan(f"yi{i}") for i in range(2)]
            xi, xich = [Buf(P.sb(f"xi{i}", [128, NK, 128])) for i in range(2)], [P.chan(f"xi{i}") for i in range(2)]
        zi = [Buf(P.sb(f"zi{i}", [128, N])) for i in range(nb)]
        zich = [P.chan(f"zi{i}") for i in range(nb)]
        ai = [Buf(P.sb(f"ai{i}", [128, N])) for i in range(nb)]
        aich = [P.chan(f"ai{i}") for i in range(nb)]
        zch = [P.chan(f"z{i}") for i in range(2)]
        a2s = [Buf(P.sb(f"a2{i}", [128, N])) for i in range(2)] if sums else None
        a2ch = [P.chan(f"a2{i}") for i in range(2)]
        tok = {}

        def load(n):
            i, g = n % nb, order[n]
            tok[n] = [P.dma("sp", zich[i], zi[i].t[:], S[f"z{l - 1}"][g], zi[i].free),
                      P.dma("sp", aich[i], ai[i].t[:], S[f"ag{l - 1}"][g], ai[i].free)]
            if not sums:
                i = n % 2
                yi[i].ready = P.dma("sp", yich[i], yi[i].t[:], S["z1"][g], yi[i].free)
                xi[i].ready = P.dma("sp", xich[i], flat2(xi[i].t), S["x1"][g], xi[i].free)
            elif n < G - 3:
                sg.load_keep(n)
                sg.load_adj(n)

        def norm(n):
            tok[n].append(affine(P, C, l - 1, zi[n % nb].t[:], tok[n], pool=not sums))
            if not sums:
                yi[n % 2].ready = affine(P, C, 1, yi[n % 2].t[:], yi[n % 2].ready, pool=True)

        def layer(n, between=None):
            i = n % nb
            a, b = dn.products(ai[i].t, zi[i].t, C["W"][:, 1 + 2 * l, :], C["W"][:, 2 + 2 * l, :], tok[n],
                               second_first=not sums)
            ai[i].free, zi[i].free = [a], [b]
            dn.rows(n, C["rows"][:, 2 + l, :], C["rows"][:, 6, :], between)

        def out_product(n):
            a, b = yi[n % 2], zi[n % nb]
            for k in range(NK):
                P.pe(lambda e, k=k: e.matmul(py.t[:, k, :], a.t[:, blk(k)], C["W"][:, 9, :], start=True, stop=False,
                                             skip_group_check=True), a.ready, py.free, sig=False)
                m = P.pe(lambda e, k=k: e.matmul(py.t[:, k, :], b.t[:, blk(k)], C["W"][:, 10, :], start=False, stop=True,
                                                 skip_group_check=True), tok[n], sig=(k == NK - 1))
            a.free = [m]
            b.free.append(m)
            return m

        def out_part(n, m):
            g, X = order[n], xi[n % 2]
            part = C["part"][g].rearrange("p (k d) -> p k d", d=128)
            c = P.pool(lambda e: e.tensor_tensor(part, C["rows"][:, 9, :].unsqueeze(1).to_broadcast([128, NK, 128]),
                                                 bc(col8(C["mf"], g), 128), ALU.mult))
            c = P.pool(lambda e: e.tensor_tensor(part, part, X.t[:], ALU.add), c, X.ready)
            X.free = [c]
            a = [P.act(lambda e, k=k: e.activation(yy.t[:, k, :], py.t[:, k, :], ACT.Copy,
                                                   scale=C["mf2"][:, g * NK + k:g * NK + k + 1]), m, yy.free)
                 for k in range(NK)]
            py.free = [a[-1]]
            t = P.pool(lambda e: e.tensor_tensor(part, part, yy.t[:], ALU.add), c, a)
            yy.free = [t]

        def turn(n):
            dn.turn(n, stats)
            if sums:
                zT = dn.zT(n)
                zT.free.append(P.dma("sp", zch[n % 2], S["z2"][order[n]], zT.t[:], zT.ready))

        load(run[0])
        load(run[1])
        norm(run[0])
        last = None
        for t, n in enumerate([*run, None]):
            if sums:
                if last is not None:
                    turn(last)
                    z, a2 = dn.z[last % 2], a2s[last % 2]
                if n is not None:
                    layer(n)
                if last is not None:
                    sg.agg(last, z.t, z.ready, (0,))
                    sg.evac(a2.t, a2.free, (0,))
                if n is not None:
                    if n < G - 3:
                        sg.mask(n)
                if last is not None:
                    e = sg.agg(last, z.t, z.ready, (1,))
                    z.free.append(e)
                    sg.adj[last % 3].free = [e]
                if t + 1 < G:
                    norm(run[t + 1])
                if last is not None:
                    e = sg.evac(a2.t, a2.free, (1,))
                    a2.free = [P.dma("sp", a2ch[last % 2], S["ag2"][order[last]], a2.t[:], e)]
            else:
                if t + 1 < G:
                    norm(run[t + 1])
                if n is not None:
                    m = []

                    def between(n=n, last=last):
                        if last is not None:
                            turn(last)
                        m.append(out_product(n))
                    layer(n, between)
                    out_part(n, m[0])
                else:
                    turn(last)
            if t + 2 < G:
                load(run[t + 2])
            last = n
        fold(P, C, stats, l, st_all(P, dn))
        P.run()


def final(nc, A, C, S):
    with ExitStack() as ctx:
        P = Phase(nc, ctx, "f")
        och = P.chan("o")
        pp = [Buf(P.ps(f"p{i}", [128, NK, 128])) for i in range(4)]
        for g in range(G):
            p = pp[g % 4]
            h = affine(P, C, 3, C["z3"][g])
            for k in range(NK):
                m = P.pe(lambda e, k=k, g=g, p=p: e.matmul(p.t[:, k, :], C["z3"][g][:, blk(k)], C["W"][:, 11, :], start=True,
                                                           stop=True), h, p.free, sig=(k == NK - 1))
            for k in range(NK):
                c = P.dve(lambda e, k=k, g=g, p=p: e.scalar_tensor_tensor(
                    C["part"][g][:, blk(k)], p.t[:, k, :], C["mf2"][:, g * NK + k:g * NK + k + 1],
                    C["part"][g][:, blk(k)], ALU.mult, ALU.add), m)
            p.free = [c]
            P.dma("sp", och, A["out"][g], C["part"][g], c)
        P.run()


def kernel(**inputs):
    import concourse.bacc as bacc
    from concourse.bass_utils import run_bass_kernel_spmd as run

    I = {k: np.asarray(v) for k, v in inputs.items()}
    adj = np.ascontiguousarray(I["adj"])
    arrays = {
        "x": np.ascontiguousarray(I["x"].reshape(G, NK, 128, D).transpose(0, 2, 1, 3).reshape(G, 128, N)),
        "adj": adj,
        "adjT": np.ascontiguousarray(adj.transpose(0, 2, 1)),
        "mask": np.ascontiguousarray(I["nodemask"].reshape(G, NK, 128).transpose(2, 0, 1).reshape(128, G * NK)),
    }
    wl = I["L1_gnn_Wl"]
    W = [I["L0_gnn_W0"], I["L0_gnn_W1"], I["L0_gnn_W2"], I["L1_gnn_Wr1"], I["L1_gnn_Wx1"], I["L1_gnn_Wr2"],
         I["L1_gnn_Wx2"], I["L1_gnn_Wr3"], I["L1_gnn_Wx3"], wl[0:128], wl[128:256], wl[256:384]]
    arrays["W"] = np.ascontiguousarray(np.stack(W, 1))
    z = np.zeros(128, np.float32)
    arrays["rows"] = np.ascontiguousarray(np.stack([
        I["L0_gnn_b0"], I["L0_gnn_b1"], I["L0_gnn_b2"], I["L1_gnn_b1"], I["L1_gnn_b2"], I["L1_gnn_b3"], z, z, z,
        I["L1_gnn_bl"]]))
    arrays["cols"] = np.ascontiguousarray(np.stack([
        I["L1_gnn_g1"], I["L1_gnn_be1"], I["L1_gnn_g2"], I["L1_gnn_be2"], I["L1_gnn_g3"], I["L1_gnn_be3"]], 1))
    nc = bacc.Bacc("TRN2", target_bir_lowering=False, num_devices=1)
    feed, args = {}, {}
    for name, a in arrays.items():
        feed[f"in_{name}"] = a
        args[name] = nc.dram_tensor(f"in_{name}", a.shape, mybir.dt.from_np(a.dtype), kind="ExternalInput").ap()
    args["out"] = nc.dram_tensor("out_0", (G, 128, N), F32, kind="ExternalOutput").ap()
    build(nc, args)
    r = run(nc, [feed], core_ids=[0])
    o = r.results[0]["out_0"]
    return np.ascontiguousarray(o.reshape(G, 128, NK, D).transpose(0, 2, 1, 3).reshape(G, N, D))
```
